# Optimizing a Trainium2 kernel written in Bass

```python
import numpy as np
import jax
import jax.numpy as jnp

def _softmax(x, axis=-1):
    return jax.nn.softmax(x, axis=axis)

def _gelu(x):
    return jax.nn.gelu(x, approximate=True)

def _silu(x):
    return jax.nn.silu(x)

def _sigmoid(x):
    return jax.nn.sigmoid(x)

def _layernorm(x, axis=-1, eps=1e-05):
    m = jnp.mean(x, axis=axis, keepdims=True)
    v = jnp.var(x, axis=axis, keepdims=True)
    return (x - m) / jnp.sqrt(v + eps)

def _scatter_add(tgt, idx, src, axis=0):
    return tgt.at[idx].add(src)

def _segment_sum(src, seg, n):
    return jax.ops.segment_sum(src, seg, n)
kernel_name = 'mk_flamingo_gated_d1_seqx_r2_c5b1e1'

def setup_inputs(seed: int=0):
    np.random.seed(seed)
    _w = jnp.asarray

    def _rec_inputs():
        import jax
        import jax.numpy as jnp
        _rk = jax.random.key(seed)
        x = -0.0002928 + 1 * jax.random.normal(jax.random.fold_in(_rk, 1), (32, 256, 512), jnp.float32)
        _lenS = 256 - jax.random.randint(jax.random.fold_in(_rk, 7), (32,), 0, max(1, 256 // 4) + 1, jnp.int32)
        _lenS2 = 256 - jax.random.randint(jax.random.fold_in(_rk, 8), (32,), 0, max(1, 256 // 4) + 1, jnp.int32)
        _ctx_1024P = jax.random.normal(jax.random.fold_in(_rk, 11), (32, 16, 512), jnp.float32)
        _ctx_1024c = jax.random.dirichlet(jax.random.fold_in(_rk, 511), 0.3 * jnp.ones((16,), jnp.float32), (32, 256))
        _ctx_1024t = jnp.einsum('bsk,bkd->bsd', _ctx_1024c, _ctx_1024P)
        _ctx_1024t = _ctx_1024t * jax.lax.rsqrt(jnp.mean(jnp.square(_ctx_1024t)) + 1e-12) * 0.953939
        ctx_1024 = -1.39393e-06 + 0.999914 * (_ctx_1024t + 0.3 * jax.random.normal(jax.random.fold_in(_rk, 611), (32, 256, 512), jnp.float32))
        _validS = jnp.arange(256)[None, :] < _lenS[:, None]
        _validS2 = jnp.arange(256)[None, :] < _lenS2[:, None]
        _causal = jnp.tril(jnp.ones((256, 256), dtype=bool))
        mask_BxS2_if1 = jnp.where(jnp.ones((32, 256), dtype=bool), 1, 0).astype(jnp.int32)
        _g = jax.random.normal(jax.random.fold_in(_rk, 9001), (2, 1), jnp.float32)
        _g = jnp.sign(_g) * jnp.maximum(jnp.abs(_g), 1.0) + (_g == 0) * 1.0
        g_xattn = _g[0]
        g_ffn = _g[1]
        return (x, ctx_1024, mask_BxS2_if1, g_xattn, g_ffn)
    x, ctx_1024, mask_BxS2_if1, g_xattn, g_ffn = _rec_inputs()

    def _L0_xattn_setup():
        import jax, jax.numpy as jnp
        import numpy as np
        D_MODEL = 512
        N_HEADS = 16
        HEAD_DIM = D_MODEL // N_HEADS
        ROPE_BASE = 10000.0

        def apply_rope(x):
            b, s, h, d = x.shape
            h_half = d // 2
            theta = 1.0 / ROPE_BASE ** (jnp.arange(0, d, 2, dtype=jnp.float32) / d)
            idx_theta = jnp.arange(s, dtype=jnp.float32)[:, None] * theta[None, :]
            cos = jnp.cos(idx_theta)[None, :, None, :]
            sin = jnp.sin(idx_theta)[None, :, None, :]
            xs = x.reshape(b, s, h, h_half, 2)
            x0, x1 = (xs[..., 0], xs[..., 1])
            out = jnp.stack((x0 * cos - x1 * sin, x1 * cos + x0 * sin), axis=-1)
            return out.reshape(b, s, h, d)
        key = jax.random.key(seed)
        ks = jax.random.split(key, 8)
        B, S, D = (2, 1024, D_MODEL)
        scale = 0.02
        return {'Q': jax.random.normal(ks[0], (B, S, D), dtype=jnp.float32), 'K': jax.random.normal(ks[1], (B, S, D), dtype=jnp.float32), 'V': jax.random.normal(ks[2], (B, S, D), dtype=jnp.float32), 'attention_mask': jnp.ones((B, S), dtype=jnp.int32), 'Wq': jax.random.normal(ks[3], (D, D), dtype=jnp.float32) * scale, 'Wk': jax.random.normal(ks[4], (D, D), dtype=jnp.float32) * scale, 'Wv': jax.random.normal(ks[5], (D, D), dtype=jnp.float32) * scale, 'Wo': jax.random.normal(ks[6], (D, D), dtype=jnp.float32) * scale, 'bo': jax.random.normal(ks[7], (D,), dtype=jnp.float32) * scale}
    _L0_xattn_all = _L0_xattn_setup()
    _L0_xattn_in = {k: v for k, v in _L0_xattn_all.items() if k in ('Wq', 'Wk', 'Wv', 'Wo', 'bo')}
    del _L0_xattn_all

    def _L0_ffn_setup():
        import jax, jax.numpy as jnp
        import numpy as np
        DIM = 512
        HIDDEN = 1536
        SCALE = 1.0 / 127.0

        def _dequant(w_int, dtype):
            return w_int.astype(dtype) * jnp.asarray(SCALE, dtype)
        key = jax.random.key(seed)
        k_x, k_g, k_u, k_d = jax.random.split(key, 4)
        x = jax.random.normal(k_x, (4, 1024, DIM), dtype=jnp.float32)
        w_gate = jax.random.randint(k_g, (HIDDEN, DIM), -127, 128, dtype=jnp.int32)
        w_up = jax.random.randint(k_u, (HIDDEN, DIM), -127, 128, dtype=jnp.int32)
        w_down = jax.random.randint(k_d, (DIM, HIDDEN), -127, 128, dtype=jnp.int32)
        return {'x': x, 'w_gate': w_gate, 'w_up': w_up, 'w_down': w_down}
    _L0_ffn_all = _L0_ffn_setup()
    _L0_ffn_in = {k: v for k, v in _L0_ffn_all.items() if k in ('w_gate', 'w_up', 'w_down')}
    del _L0_ffn_all
    return {'x': x, 'ctx_1024': ctx_1024, 'mask_BxS2_if1': mask_BxS2_if1, 'g_xattn': g_xattn, 'g_ffn': g_ffn, 'L0_xattn_Wq': _L0_xattn_in['Wq'], 'L0_xattn_Wk': _L0_xattn_in['Wk'], 'L0_xattn_Wv': _L0_xattn_in['Wv'], 'L0_xattn_Wo': _L0_xattn_in['Wo'], 'L0_xattn_bo': _L0_xattn_in['bo'], 'L0_ffn_w_gate': _L0_ffn_in['w_gate'], 'L0_ffn_w_up': _L0_ffn_in['w_up'], 'L0_ffn_w_down': _L0_ffn_in['w_down']}

def reference(x, ctx_1024, mask_BxS2_if1, g_xattn, g_ffn, L0_xattn_Wq, L0_xattn_Wk, L0_xattn_Wv, L0_xattn_Wo, L0_xattn_bo, L0_ffn_w_gate, L0_ffn_w_up, L0_ffn_w_down):
    import jax
    import jax.numpy as jnp

    def _L0_xattn_ref(Q, K, V, attention_mask, Wq, Wk, Wv, Wo, bo):
        import jax, jax.numpy as jnp
        import numpy as np
        D_MODEL = 512
        N_HEADS = 16
        HEAD_DIM = D_MODEL // N_HEADS
        ROPE_BASE = 10000.0

        def apply_rope(x):
            b, s, h, d = x.shape
            h_half = d // 2
            theta = 1.0 / ROPE_BASE ** (jnp.arange(0, d, 2, dtype=jnp.float32) / d)
            idx_theta = jnp.arange(s, dtype=jnp.float32)[:, None] * theta[None, :]
            cos = jnp.cos(idx_theta)[None, :, None, :]
            sin = jnp.sin(idx_theta)[None, :, None, :]
            xs = x.reshape(b, s, h, h_half, 2)
            x0, x1 = (xs[..., 0], xs[..., 1])
            out = jnp.stack((x0 * cos - x1 * sin, x1 * cos + x0 * sin), axis=-1)
            return out.reshape(b, s, h, d)
        b, s, d = Q.shape
        q = (Q @ Wq.T).reshape(b, s, N_HEADS, HEAD_DIM)
        k = (K @ Wk.T).reshape(b, s, N_HEADS, HEAD_DIM)
        v = (V @ Wv.T).reshape(b, s, N_HEADS, HEAD_DIM)
        q = apply_rope(q)
        k = apply_rope(k)
        scores = jnp.einsum('bnhd,bmhd->bhnm', q, k) / jnp.sqrt(jnp.float32(HEAD_DIM))
        pad = (attention_mask != 0)[:, None, None, :]
        scores = jnp.where(pad, scores, -jnp.inf)
        causal = jnp.tril(jnp.ones((s, s), dtype=bool))[None, None]
        scores = jnp.where(causal, scores, -jnp.inf)
        attn = jax.nn.softmax(scores, axis=-1)
        out = jnp.einsum('bhnm,bmhd->bnhd', attn, v).reshape(b, s, d)
        return out @ Wo.T + bo

    def _L0_ffn_ref(x, w_gate, w_up, w_down):
        import jax, jax.numpy as jnp
        import numpy as np
        DIM = 512
        HIDDEN = 1536
        SCALE = 1.0 / 127.0

        def _dequant(w_int, dtype):
            return w_int.astype(dtype) * jnp.asarray(SCALE, dtype)
        wg = _dequant(w_gate, x.dtype)
        wu = _dequant(w_up, x.dtype)
        wd = _dequant(w_down, x.dtype)
        gate = jnp.einsum('bsd,hd->bsh', x, wg)
        up = jnp.einsum('bsd,hd->bsh', x, wu)
        h = jax.nn.silu(gate) * up
        return jnp.einsum('bsh,dh->bsd', h, wd)
    x = x + jnp.tanh(g_xattn[0]) * _L0_xattn_ref(_layernorm(x, axis=-1), ctx_1024, ctx_1024, mask_BxS2_if1, L0_xattn_Wq, L0_xattn_Wk, L0_xattn_Wv, L0_xattn_Wo, L0_xattn_bo)
    x = x + jnp.tanh(g_ffn[0]) * _L0_ffn_ref(_layernorm(x, axis=-1), L0_ffn_w_gate, L0_ffn_w_up, L0_ffn_w_down)
    return x

_drawn_inputs = setup_inputs


def setup_inputs(seed=0):
    import zlib

    import numpy as np

    out = dict(_drawn_inputs(seed))
    spreads = {}
    factors = {'L0_xattn_Wq': 7.552, 'L0_xattn_Wk': 7.536, 'L0_xattn_bo': 2.679}
    for name, (base, spread) in spreads.items():
        noise = np.random.default_rng([zlib.crc32(name.encode()), seed]).standard_normal(out[name].shape)
        drawn = base * np.exp(spread * noise) if base else spread * noise
        out[name] = jnp.asarray(drawn.astype(out[name].dtype))
    for name, factor in factors.items():
        out[name] = (out[name] * factor).astype(out[name].dtype)
    return out
```

```python
import math
from contextlib import ExitStack

import numpy as np

import concourse.bass as bass
from concourse import mybir

F32 = mybir.dt.float32
F32R = mybir.dt.float32r
I32 = mybir.dt.int32
ALU = mybir.AluOpType
ACT = mybir.ActivationFunctionType
AX = mybir.AxisListType

P = 128
B, S, D = 32, 256, 512
H, DH = 16, 32
HID = 1536
TT = S // P
KT = D // P
HG = P // DH
HT = HID // P
EPS = 1e-5
SCALE = 1.0 / math.sqrt(DH)
DEQ = float(np.float32(1.0 / 127.0))
STACK = 3 * DH
STACK_DMAS = 3 * HG
ROPE_BASE = 10000.0
BIG = 1.0e30


class Batch:

    def __init__(self, j, c):
        self.j, self.c = j, c

    def __add__(self, d):
        return Batch(self.j + (self.c + d) // 2 if (self.c + d) // 2 else self.j, (self.c + d) % 2)

    @property
    def row(self):
        return self.j * 2 + self.c

    @property
    def exists(self):
        return not isinstance(self.j, int) or 0 <= self.row < B

    def count(self, per_row, n):
        value = self.row * per_row + n
        return max(value, 0) if isinstance(value, int) else value

    def half_count(self, n):
        return self.j * n + n


def each_batch(eng, body):
    for c in range(2):
        body(Batch(0, c))
    with eng.Fori(1, B // 2 - 1) as j:
        for c in range(2):
            body(Batch(j, c))
    for c in range(2):
        body(Batch(B // 2 - 1, c))


def attention_phase(nc, x, ctx_t, mask, g_xattn, wq_t, wk_t, wv_t, wo_t, bo, cos, sin, causal, ident, x2_dram):
    with ExitStack() as ctx:
        def sb(name, shape, dt=F32):
            return ctx.enter_context(nc.sbuf_tensor(name, shape, dt))

        def pb(name):
            return ctx.enter_context(nc.psum_tensor(name, [P, 512], F32))

        def sem(name):
            return ctx.enter_context(nc.semaphore(name))

        weights = {"k": wk_t, "q": wq_t, "v": wv_t, "o": wo_t}
        w_hi = {n: sb(f"w{n}_hi", [P, KT, D], F32R) for n in weights}
        w_lo = {n: sb(f"w{n}_lo", [P, KT, D], F32R) for n in weights}
        identity = sb("identity", [P, P])
        cos_sb = sb("cos_sb", [P, TT, DH])
        sin_sb = sb("sin_sb", [P, TT, DH])
        causal_sb = sb("causal_sb", [P, 3 * P])
        gate = sb("gate", [P, 1])
        gate_bo = sb("gate_bo", [P, D])
        x_raw = sb("x_raw", [P, 2, TT, D])
        x_res = sb("x_res", [P, TT, D])
        xn = sb("xn", [P, TT, D])
        xnt_hi = sb("xnt_hi", [P, KT, S], F32R)
        xnt_lo = sb("xnt_lo", [P, KT, S], F32R)
        ctx_raw = sb("ctx_raw", [P, KT, S])
        ctx_hi = sb("ctx_hi", [P, KT, S], F32R)
        ctx_lo = sb("ctx_lo", [P, KT, S], F32R)
        stats = sb("stats", [P, TT, 6])
        moments = sb("moments", [P, TT, 2])
        var_eps = sb("var_eps", [P, TT])
        rstd = sb("rstd", [P, TT])
        minus_half = sb("minus_half", [P, TT])
        roped = {n: sb(f"{n}_roped", [P, TT, D]) for n in "qk"}
        rope_sin = sb("rope_sin", [P, D])
        qt_hi = sb("qt_hi", [P, KT, S], F32R)
        qt_lo = sb("qt_lo", [P, KT, S], F32R)
        kt_hi = sb("kt_hi", [P, KT, S], F32R)
        kt_lo = sb("kt_lo", [P, KT, S], F32R)
        q_stack = sb("q_stack", [STACK, H, S], F32R)
        k_stack = sb("k_stack", [STACK, 2, H, S], F32R)
        v_sb = sb("v_sb", [P, TT, D])
        mask_int = sb("mask_int", [P, S], I32)
        pad = sb("pad", [P, S])
        mask_sb = sb("mask_sb", [P, 2, 3 * P])
        prob = sb("prob", [P, 4, 3 * P])
        neg_max = sb("neg_max", [P, 4, TT])
        row_sum = sb("row_sum", [P, 4, TT])
        row_rcp = sb("row_rcp", [P, 4, TT])
        probt = sb("probt", [P, 2, 3 * P])
        ot_hi = sb("ot_hi", [P, KT, S], F32R)
        ot_lo = sb("ot_lo", [P, KT, S], F32R)

        proj_ps = [pb(f"proj_ps{t}") for t in range(TT)]
        tr_ps = pb("tr_ps")
        score_ps = [pb(f"score_ps{n}") for n in range(2)]
        probt_ps = pb("probt_ps")
        out_ps = [pb(f"out_ps{n}") for n in range(2)]

        consts_loaded = sem("consts_loaded")
        weight_loaded = sem("weight_loaded")
        weight_rounded = sem("weight_rounded")
        weight_split = sem("weight_split")
        gate_ready = sem("gate_ready")
        gate_bo_ready = sem("gate_bo_ready")
        half_ready = sem("half_ready")
        x_loaded = [sem(f"x_loaded{p}") for p in range(2)]
        ctx_loaded = sem("ctx_loaded")
        mask_loaded = sem("mask_loaded")
        ctx_rounded = sem("ctx_rounded")
        ctx_split = sem("ctx_split")
        res_ready = sem("res_ready")
        stats_ready = sem("stats_ready")
        moments_ready = sem("moments_ready")
        var_ready = sem("var_ready")
        rstd_ready = sem("rstd_ready")
        xn_ready = sem("xn_ready")
        pad_ready = sem("pad_ready")
        mask_ready = sem("mask_ready")
        projected = {n: sem(f"{n}_projected") for n in "qkvo"}
        transposed = {n: sem(f"{n}_transposed") for n in "xqk"}
        rounded = {n: sem(f"{n}_rounded") for n in "xqk"}
        split = {n: sem(f"{n}_split") for n in "xqk"}
        rope_read = {n: sem(f"{n}_rope_read") for n in "qk"}
        rope_added = {n: sem(f"{n}_rope_added") for n in "qk"}
        stacked = {n: sem(f"{n}_stacked") for n in "qk"}
        v_copied = sem("v_copied")
        scored = sem("scored")
        masked = sem("masked")
        exp_done = sem("exp_done")
        rcp_done = sem("rcp_done")
        normed = sem("normed")
        prob_transposed = sem("prob_transposed")
        probt_copied = sem("probt_copied")
        pv_done = sem("pv_done")
        out_rounded = sem("out_rounded")
        out_split = sem("out_split")
        x2_ready = sem("x2_ready")
        x2_stored = sem("x2_stored")

        CONSTS = 6
        block = ctx.enter_context(nc.Block())

        @block.sync
        def _(sp):
            for dst, src in ((identity, ident), (cos_sb, cos), (sin_sb, sin), (causal_sb, causal)):
                sp.dma_start(dst[:], src).then_inc(consts_loaded, 16)
            sp.dma_start(gate[:, :], g_xattn.to_broadcast([P, 1])).then_inc(consts_loaded, 16)
            sp.dma_start(gate_bo[:, :], bo.to_broadcast([P, D])).then_inc(consts_loaded, 16)
            sp.dma_start(mask_int[:, :], mask[0:1, :].to_broadcast([P, S])).then_inc(mask_loaded, 16)
            for n, w in enumerate(weights.values()):
                if n:
                    sp.wait_ge(weight_split, n)
                sp.dma_start(x_raw[:, :, :, :], w.rearrange("(k p) n -> p k n", p=P)
                             .rearrange("p (a b) n -> p a b n", a=2)).then_inc(weight_loaded, 16)
                if n == 0:
                    sp.dma_start(ctx_raw[:, :, :], ctx_t[0].rearrange("(k p) s -> p k s", p=P)).then_inc(ctx_loaded, 16)
            sp.wait_ge(weight_split, len(weights))

            def load_x(b):
                if b.exists:
                    sp.dma_start(x_raw[:, b.c, :, :], x[b.row].rearrange("(t p) d -> p t d", p=P)).then_inc(x_loaded[b.c], 16)

            def load_ctx(b):
                if b.exists:
                    sp.wait_ge(ctx_split, b.count(1, 0))
                    sp.dma_start(ctx_raw[:, :, :], ctx_t[b.row].rearrange("(k p) s -> p k s", p=P)).then_inc(ctx_loaded, 16)

            def load_mask(b):
                if b.exists:
                    sp.wait_ge(pad_ready, b.count(1, 0))
                    sp.dma_start(mask_int[:, :], mask[bass.ds(b.row, 1), :].to_broadcast([P, S])).then_inc(mask_loaded, 16)

            def stack(name, b, dst, hi, lo, order):
                sp.wait_ge(split[name], b.count(2, 2))
                for block_no, part in enumerate(order):
                    src = hi if part == "hi" else lo
                    for q in range(HG):
                        sp.dma_start(dst[block_no * DH:(block_no + 1) * DH, :, q, :].bitcast(F32),
                                     src[q * DH:(q + 1) * DH, :, :].bitcast(F32)).then_inc(stacked[name], 16)

            def stack_k(b):
                sp.wait_ge(scored, (b + -2).count(H, H))
                stack("k", b, k_stack[:, b.c, :, :].rearrange("r (t q) s -> r t q s", q=HG), kt_hi, kt_lo, ("hi", "lo", "hi"))

            def stack_q(b):
                sp.wait_ge(scored, b.count(H, 0))
                stack("q", b, q_stack[:, :, :].rearrange("r (t q) s -> r t q s", q=HG), qt_hi, qt_lo, ("hi", "hi", "lo"))

            def store_x2(b):
                sp.wait_ge(x2_ready, b.count(TT, TT))
                sp.dma_start(x2_dram[b.row].rearrange("(t p) d -> p t d", p=P), x_res[:, :, :]).then_inc(x2_stored, 16)

            load_x(Batch(0, 0))
            load_x(Batch(0, 1))
            load_ctx(Batch(0, 1))
            load_mask(Batch(0, 1))
            stack_k(Batch(0, 0))
            stack_q(Batch(0, 0))

            def body(b):
                if (b + -1).exists:
                    store_x2(b + -1)
                if (b + 2).exists:
                    sp.wait_ge(res_ready, b.count(1, 1))
                    load_x(b + 2)
                    load_ctx(b + 2)
                    load_mask(b + 2)
                if (b + 1).exists:
                    stack_k(b + 1)
                    stack_q(b + 1)

            each_batch(sp, body)
            store_x2(Batch(B // 2 - 1, 1))
            sp.wait_ge(x2_stored, 16 * B)

        @block.gpsimd
        def _(pool):
            nc.gpsimd.memset(minus_half[:, :], -0.5).then_inc(half_ready, 1)
            pool.wait_ge(half_ready, 1)

            def split_ctx(b):
                if b.exists:
                    pool.wait_ge(projected["v"], b.count(TT, 0))
                    pool.wait_ge(ctx_rounded, b.count(1, 1))
                    nc.gpsimd.tensor_tensor(ctx_lo[:, :, :], ctx_raw[:, :, :], ctx_hi[:, :, :].bitcast(F32),
                                            ALU.subtract).then_inc(ctx_split, 1)

            def inverse_std(b):
                if b.exists:
                    pool.wait_ge(xn_ready, b.count(TT, 0))
                    pool.wait_ge(var_ready, b.count(1, 1))
                    nc.gpsimd.tensor_tensor(rstd[:, :], var_eps[:, :], minus_half[:, :], ALU.pow).then_inc(rstd_ready, 1)

            def rope_add(name, b):
                if b.exists:
                    for t in range(TT):
                        pool.wait_ge(rope_read[name], b.count(TT, t + 1))
                        nc.gpsimd.tensor_tensor(roped[name][:, t, :], roped[name][:, t, :], rope_sin[:, :], ALU.add).then_inc(rope_added[name], 1)

            def residual(b):
                pool.wait_ge(x_loaded[b.c], b.half_count(16))
                pool.wait_ge(x2_stored, b.count(16, 0))
                pool.wait_ge(gate_bo_ready, 2)
                for t in range(TT):
                    last = nc.gpsimd.tensor_tensor(x_res[:, t, :], x_raw[:, b.c, t, :], gate_bo[:, :], ALU.add)
                last.then_inc(res_ready, 1)

            first = Batch(0, 0)
            split_ctx(first)
            inverse_std(first)
            rope_add("k", first)
            rope_add("q", first)
            inverse_std(first + 1)
            split_ctx(first + 1)

            def body(b):
                residual(b)
                rope_add("k", b + 1)
                rope_add("q", b + 1)
                inverse_std(b + 2)
                split_ctx(b + 2)

            each_batch(pool, body)

        @block.scalar
        def _(act):
            act.wait_ge(consts_loaded, 16 * CONSTS)
            nc.scalar.activation(gate[:, :], gate[:, :], ACT.Tanh).then_inc(gate_ready, 1)

            def exponentials(b, h):
                n = h % 4
                act.wait_ge(masked, b.count(H, h + 1))
                for t, (lo, hi) in enumerate(((0, P), (P, 3 * P))):
                    last = nc.scalar.activation(prob[:, n, lo:hi], prob[:, n, lo:hi], ACT.Exp, bias=neg_max[:, n, t:t + 1],
                                                scale=-1.0, accum_out=row_sum[:, n, t:t + 1])
                last.then_inc(exp_done, 1)

            def copy_probt(b, h):
                act.wait_ge(pv_done, b.count(H, h - 1))
                act.wait_ge(prob_transposed, b.count(H, h + 1))
                nc.scalar.activation(probt[:, h % 2, :], probt_ps[:, 0:3 * P], ACT.Copy).then_inc(probt_copied, 1)

            def round_transposed(name, b, u, dst):
                if b.exists:
                    if name == "x":
                        act.wait_ge(projected["q"], b.count(TT, 0))
                    else:
                        act.wait_ge(stacked[name], b.count(16 * STACK_DMAS, 0))
                    act.wait_ge(transposed[name], b.count(2, u + 1))
                    nc.scalar.activation(dst[:, 2 * u:2 * u + 2, :], tr_ps[:, :].rearrange("p (k s) -> p k s", k=2),
                                         ACT.Copy).then_inc(rounded[name], 1)

            def copy_v(b, t):
                if b.exists:
                    act.wait_ge(pv_done, b.count(H, 0))
                    act.wait_ge(projected["v"], b.count(TT, t + 1))
                    nc.scalar.activation(v_sb[:, t, :], proj_ps[t][:, :], ACT.Copy).then_inc(v_copied, 1)

            def round_out(b, g):
                act.wait_ge(projected["o"], b.count(TT, 0))
                act.wait_ge(pv_done, b.count(H, HG * g + HG))
                nc.scalar.activation(ot_hi[:, g, :], out_ps[g % 2][:, 0:S], ACT.Copy).then_inc(out_rounded, 1)

            first = Batch(0, 0)
            for u in range(2):
                round_transposed("x", first, u, xnt_hi)
            for u in range(2):
                round_transposed("k", first, u, kt_hi)
            for u in range(2):
                round_transposed("q", first, u, qt_hi)
            for t in range(TT):
                copy_v(first, t)
            for u in range(2):
                round_transposed("x", first + 1, u, xnt_hi)

            def body(b):
                for s in range(H + 4):
                    if s >= 4:
                        copy_probt(b, s - 4)
                    if s < H:
                        exponentials(b, s)
                    if s in (7, 9):
                        round_transposed("k", b + 1, (s - 7) // 2, kt_hi)
                    if s in (11, 13):
                        round_transposed("q", b + 1, (s - 11) // 2, qt_hi)
                    if s in (9, 13, 17):
                        round_out(b, s // 4 - 2)
                round_out(b, KT - 1)
                for t in range(TT):
                    copy_v(b + 1, t)
                for u in range(2):
                    round_transposed("x", b + 2, u, xnt_hi)

            each_batch(act, body)

        @block.vector
        def _(dve):
            dve.wait_ge(gate_ready, 1)
            nc.vector.tensor_scalar(gate_bo[:, :], gate_bo[:, :], gate[:, 0:1], None, ALU.mult).then_inc(gate_bo_ready, 2)
            for n, name in enumerate(weights):
                dve.wait_ge(weight_loaded, 16 * (n + 1))
                stage = x_raw[:, :, :, :].rearrange("p a b n -> p (a b) n")
                nc.vector.tensor_copy(w_hi[name][:, :, :], stage).then_inc(weight_rounded, 1)
                dve.wait_ge(weight_rounded, n + 1)
                nc.vector.tensor_tensor(w_lo[name][:, :, :], stage, w_hi[name][:, :, :].bitcast(F32),
                                        ALU.subtract).then_inc(weight_split, 1)

            def statistics(b):
                if b.exists:
                    dve.wait_ge(x_loaded[b.c], b.half_count(16))
                    for t in range(TT):
                        last = nc.vector.bn_stats(stats[:, t, :], x_raw[:, b.c, t, :])
                    last.then_inc(stats_ready, 1)

            def statistics_there(b):
                if b.exists:
                    dve.wait_ge(stats_ready, b.count(1, 1))

            def variance(b):
                if b.exists:
                    for t in range(TT):
                        last = nc.vector.bn_aggr(moments[:, t, :], stats[:, t, :])
                    last.then_inc(moments_ready, 1)
                    dve.wait_ge(moments_ready, b.count(1, 1))
                    nc.vector.tensor_scalar(var_eps[:, :], moments[:, :, 1], EPS, None, ALU.add).then_inc(var_ready, 1)

            def normalise(b):
                if b.exists:
                    dve.wait_ge(transposed["x"], b.count(2, 0))
                    dve.wait_ge(rstd_ready, b.count(1, 1))
                    for t in range(TT):
                        nc.vector.tensor_scalar(xn[:, t, :], x_raw[:, b.c, t, :], moments[:, t, 0:1], rstd[:, t:t + 1],
                                                ALU.subtract, ALU.mult).then_inc(xn_ready, 1)

            def split_transposed(name, b, u, hi, lo):
                if b.exists:
                    dve.wait_ge(rounded[name], b.count(2, u + 1))
                    nc.vector.tensor_tensor(lo[:, 2 * u:2 * u + 2, :], tr_ps[:, :].rearrange("p (k s) -> p k s", k=2),
                                            hi[:, 2 * u:2 * u + 2, :].bitcast(F32), ALU.subtract).then_inc(split[name], 1)

            def rope(name, b, t):
                if b.exists:
                    if t:
                        dve.wait_ge(rope_added[name], b.count(TT, t))
                    elif name == "q":
                        dve.wait_ge(rope_added["k"], b.count(TT, TT))
                    else:
                        dve.wait_ge(rope_added["q"], b.count(TT, 0))
                    dve.wait_ge(transposed[name], b.count(2, 0))
                    dve.wait_ge(projected[name], b.count(TT, t + 1))
                    table = cos_sb[:, t, :].unsqueeze(1).to_broadcast([P, H, DH])
                    nc.vector.tensor_tensor(roped[name][:, t, :].rearrange("p (h d) -> p h d", h=H),
                                            proj_ps[t][:, :].rearrange("p (h d) -> p h d", h=H), table, ALU.mult)
                    for e in range(2):
                        pairs = proj_ps[t][:, :].rearrange("p (h i e) -> p h i e", h=H, e=2)
                        signs = sin_sb[:, t, :].rearrange("p (i e) -> p i e", e=2)[:, :, e].unsqueeze(1).to_broadcast([P, H, DH // 2])
                        last = nc.vector.tensor_tensor(rope_sin[:, :].rearrange("p (h i e) -> p h i e", h=H, e=2)[:, :, :, e],
                                                       pairs[:, :, :, 1 - e], signs, ALU.mult)
                    last.then_inc(rope_read[name], 1)

            def round_ctx(b):
                if b.exists:
                    dve.wait_ge(projected["v"], b.count(TT, 0))
                    dve.wait_ge(ctx_loaded, b.count(16, 16))
                    nc.vector.tensor_copy(ctx_hi[:, :, :], ctx_raw[:, :, :]).then_inc(ctx_rounded, 1)

            def padding(b):
                if b.exists:
                    dve.wait_ge(mask_loaded, b.count(16, 16))
                    nc.vector.tensor_scalar(pad[:, :], mask_int[:, :], 0.0, -BIG, ALU.is_equal, ALU.mult).then_inc(pad_ready, 1)

            def build_mask(b):
                if b.exists:
                    dve.wait_ge(pad_ready, b.count(1, 1))
                    for lo, hi in ((0, P), (P, 3 * P)):
                        last = nc.vector.scalar_tensor_tensor(mask_sb[:, b.c, lo:hi], pad[:, 0:hi - lo], 1.0,
                                                              causal_sb[:, lo:hi], ALU.mult, ALU.add)
                    last.then_inc(mask_ready, 1)

            def scores_there(b, h):
                dve.wait_ge(prob_transposed, b.count(H, h - 3))
                dve.wait_ge(scored, b.count(H, h + 1))

            def mask_scores(b, h):
                n = h % 4
                for t, (lo, hi) in enumerate(((0, P), (P, 3 * P))):
                    last = nc.vector.tensor_tensor_reduce(out=prob[:, n, lo:hi], in0=score_ps[h % 2][:, lo:hi],
                                                          in1=mask_sb[:, b.c, lo:hi], scale=-SCALE, scalar=3.0e38, op0=ALU.add,
                                                          op1=ALU.min, accum_out=neg_max[:, n, t:t + 1])
                last.then_inc(masked, 1)

            def reciprocal_sum(b, h):
                dve.wait_ge(exp_done, b.count(H, h + 1))
                nc.vector.reciprocal(row_rcp[:, h % 4, :], row_sum[:, h % 4, :]).then_inc(rcp_done, 1)

            def normalise_probs(b, h):
                n = h % 4
                dve.wait_ge(rcp_done, b.count(H, h + 1))
                for t, (lo, hi) in enumerate(((0, P), (P, 3 * P))):
                    last = nc.vector.tensor_scalar(prob[:, n, lo:hi], prob[:, n, lo:hi], row_rcp[:, n, t:t + 1], None, ALU.mult)
                last.then_inc(normed, 1)

            def split_out(b, g):
                dve.wait_ge(out_rounded, b.count(KT, g + 1))
                nc.vector.tensor_tensor(ot_lo[:, g, :], out_ps[g % 2][:, 0:S], ot_hi[:, g, :].bitcast(F32),
                                        ALU.subtract).then_inc(out_split, 1)

            def add_residual(b, t):
                dve.wait_ge(res_ready, b.count(1, 1))
                dve.wait_ge(projected["o"], b.count(TT, t + 1))
                nc.vector.scalar_tensor_tensor(x_res[:, t, :], proj_ps[t][:, :], gate[:, 0:1], x_res[:, t, :],
                                               ALU.mult, ALU.add).then_inc(x2_ready, 1)

            first = Batch(0, 0)
            dve.wait_ge(consts_loaded, 16 * CONSTS)
            round_ctx(first)
            statistics(first)
            padding(first)
            statistics_there(first)
            variance(first)
            normalise(first)
            for u in range(2):
                split_transposed("x", first, u, xnt_hi, xnt_lo)
            build_mask(first)
            for name in "kq":
                for t in range(TT):
                    rope(name, first, t)
            for u in range(2):
                split_transposed("k", first, u, kt_hi, kt_lo)
            statistics(first + 1)
            for u in range(2):
                split_transposed("q", first, u, qt_hi, qt_lo)
            statistics_there(first + 1)
            variance(first + 1)
            round_ctx(first + 1)
            normalise(first + 1)
            for u in range(2):
                split_transposed("x", first + 1, u, xnt_hi, xnt_lo)

            def body(b):
                for s in range(H + 2):
                    if s < H:
                        scores_there(b, s)
                    if s == 11:
                        statistics_there(b + 2)
                    if s == 0:
                        padding(b + 1)
                    elif s == 1:
                        build_mask(b + 1)
                    else:
                        normalise_probs(b, s - 2)
                    if s < H:
                        mask_scores(b, s)
                    if s == 11:
                        variance(b + 2)
                    if 1 <= s <= H:
                        reciprocal_sum(b, s - 1)
                    if s in (2, 4):
                        rope("k", b + 1, s // 2 - 1)
                    if s in (6, 9):
                        rope("q", b + 1, s // 3 - 2)
                    if s == 10:
                        statistics(b + 2)
                    if s in (8, 10):
                        split_transposed("k", b + 1, (s - 8) // 2, kt_hi, kt_lo)
                    if s in (12, 14):
                        split_transposed("q", b + 1, (s - 12) // 2, qt_hi, qt_lo)
                    if s in (10, 14):
                        split_out(b, s // 4 - 2)
                    if s == 14:
                        normalise(b + 2)
                split_out(b, KT - 2)
                split_out(b, KT - 1)
                round_ctx(b + 2)
                for t in range(TT):
                    split_transposed("x", b + 2, t, xnt_hi, xnt_lo)
                    add_residual(b, t)

            each_batch(dve, body)

        @block.tensor
        def _(pe):
            def passes(out, hi, lo, w, halves):
                steps = [(st, mv, k) for k in range(KT)
                         for st, mv in ((hi, w_hi[w]), (hi, w_lo[w]), (lo, w_hi[w]))]
                n = len(steps)
                at = {"first": range(n // 2), "second": range(n // 2, n), "all": range(n)}[halves]
                for i in at:
                    st, mv, k = steps[i]
                    last = nc.tensor.matmul(out[:, :], st(k), mv[:, k, :], start=(i == 0), stop=(i == n - 1))
                return last

            def project(name, b, t, halves="all"):
                if not b.exists:
                    return
                if halves != "second":
                    if name == "k":
                        pe.wait_ge(weight_split, 1)
                        pe.wait_ge(ctx_split, b.count(1, 1))
                        pe.wait_ge(x2_ready, (b + -2).count(TT, t + 1))
                    elif name == "q":
                        pe.wait_ge(weight_split, 2)
                        pe.wait_ge(split["x"], b.count(2, 2))
                        pe.wait_ge(rope_read["k"], b.count(TT, t + 1))
                    elif name == "v":
                        pe.wait_ge(weight_split, 3)
                        pe.wait_ge(rope_read["q"], b.count(TT, t + 1))
                    else:
                        pe.wait_ge(weight_split, 4)
                        pe.wait_ge(out_split, b.count(KT, KT))
                        if (b + 1).exists:
                            pe.wait_ge(v_copied, (b + 1).count(TT, t + 1))
                        else:
                            pe.wait_ge(v_copied, b.count(TT, t + 1))
                src = {"q": (xnt_hi, xnt_lo), "k": (ctx_hi, ctx_lo), "v": (ctx_hi, ctx_lo), "o": (ot_hi, ot_lo)}[name]
                hi, lo = ((lambda k, a=a: a[:, k, t * P:(t + 1) * P]) for a in src)
                last = passes(proj_ps[t], hi, lo, name, halves)
                if halves != "first":
                    last.then_inc(projected[name], 1)

            def transpose(name, b, u):
                if not b.exists:
                    return
                if name == "x":
                    pe.wait_ge(split["x"] if u else split["q"], b.count(2, u) if u else b.count(2, 0))
                    pe.wait_ge(xn_ready, b.count(TT, TT))
                    src = xn
                else:
                    before = {"k": "x", "q": "k"}[name]
                    pe.wait_ge(split[name] if u else split[before], b.count(2, 1) if u else b.count(2, 2))
                    pe.wait_ge(rope_added[name], b.count(TT, TT))
                    src = roped[name]
                for k in range(2):
                    for t in range(TT):
                        at = (k * TT + t) * P
                        last = nc.tensor.transpose(tr_ps[:, at:at + P], src[:, t, (2 * u + k) * P:(2 * u + k + 1) * P],
                                                   identity[:, :])
                last.then_inc(transposed[name], 1)

            def score(b, h):
                if h == 0:
                    pe.wait_ge(stacked["q"], b.count(16 * STACK_DMAS, 16 * STACK_DMAS))
                    pe.wait_ge(stacked["k"], b.count(16 * STACK_DMAS, 16 * STACK_DMAS))
                pe.wait_ge(masked, b.count(H, h - 1))
                bank = score_ps[h % 2]
                nc.tensor.matmul(bank[:, 0:P], q_stack[:, h, 0:P], k_stack[:, b.c, h, 0:P], start=True, stop=True)
                nc.tensor.matmul(bank[:, P:3 * P], q_stack[:, h, P:2 * P], k_stack[:, b.c, h, :],
                                 start=True, stop=True).then_inc(scored, 1)

            def transpose_probs(b, h):
                pe.wait_ge(probt_copied, b.count(H, h))
                pe.wait_ge(normed, b.count(H, h + 1))
                for k in range(3):
                    last = nc.tensor.transpose(probt_ps[:, k * P:(k + 1) * P], prob[:, h % 4, k * P:(k + 1) * P], identity[:, :])
                last.then_inc(prob_transposed, 1)

            def product(b, h):
                g, q = divmod(h, HG)
                if q == 0:
                    pe.wait_ge(out_split, b.count(KT, g - 1))
                    pe.wait_ge(v_copied, b.count(TT, TT))
                pe.wait_ge(probt_copied, b.count(H, h + 1))
                bank = out_ps[g % 2]
                rows = slice(q * DH, (q + 1) * DH)
                nc.tensor.matmul(bank[rows, 0:S], v_sb[:, 0, h * DH:(h + 1) * DH], probt[:, h % 2, 0:S], start=True, stop=False)
                nc.tensor.matmul(bank[rows, P:S], v_sb[:, 1, h * DH:(h + 1) * DH], probt[:, h % 2, S:3 * P],
                                 start=False, stop=True).then_inc(pv_done, 1)

            first = Batch(0, 0)
            pe.wait_ge(consts_loaded, 16 * CONSTS)
            for u in range(2):
                transpose("x", first, u)
            for name in "kq":
                for t in range(TT):
                    project(name, first, t)
            for u in range(2):
                transpose("k", first, u)
            for t in range(TT):
                project("v", first, t)
            for u in range(2):
                transpose("q", first, u)
            for u in range(2):
                transpose("x", first + 1, u)

            def body(b):
                score(b, 0)
                for s in range(H + 5):
                    if s + 1 < H:
                        score(b, s + 1)
                    if s >= 5:
                        product(b, s - 5)
                    if 3 <= s < H + 3:
                        transpose_probs(b, s - 3)
                    if s in (7, 9):
                        transpose("k", b + 1, (s - 7) // 2)
                    if s in (11, 13):
                        transpose("q", b + 1, (s - 11) // 2)
                    if s < 4:
                        project("k", b + 1, s // 2, ("first", "second")[s % 2])
                    elif s < 8:
                        project("q", b + 1, s // 2 - 2, ("first", "second")[s % 2])
                    elif s in (10, 12):
                        project("v", b + 1, 0, ("first", "second")[s // 2 - 5])
                    elif s in (17, 18):
                        project("v", b + 1, 1, ("first", "second")[s - 17])
                for t in range(TT):
                    transpose("x", b + 2, t)
                    project("o", b, t)

            each_batch(pe, body)


def ffn_phase(nc, x2_dram, g_ffn, w_gate_t, w_up_t, w_down_t, ident, out_dram):
    with ExitStack() as ctx:
        def sb(name, shape, dt=F32):
            return ctx.enter_context(nc.sbuf_tensor(name, shape, dt))

        def pb(name):
            return ctx.enter_context(nc.psum_tensor(name, [P, 512], F32))

        def sem(name):
            return ctx.enter_context(nc.semaphore(name))

        WG, WU, WD = 0, 1, 2
        COLS = KT * HID
        w_hi = sb("ffn_hi", [P, 3, COLS], F32R)
        w_lo = sb("ffn_lo", [P, 3, COLS], F32R)
        CHUNK = 1024
        CHUNKS = 3 * COLS // CHUNK
        x2 = sb("x2", [P, 2, TT, D])
        xn = sb("ffn_xn", [P, TT, D])
        xt_hi = sb("ffn_xt_hi", [P, 2, KT, S], F32R)
        xt_lo = sb("ffn_xt_lo", [P, 2, KT, S], F32R)
        identity = sb("ffn_identity", [P, P])
        gate = sb("ffn_gate", [P, 1])
        stats = sb("ffn_stats", [P, TT, 6])
        moments = sb("ffn_moments", [P, TT, 2])
        var_eps = sb("ffn_var_eps", [P, TT])
        rstd = sb("ffn_rstd", [P, TT])
        minus_half = sb("ffn_minus_half", [P, TT])
        th = sb("th", [P, 2, S])
        silu2 = sb("silu2", [P, 2, S])
        hid = sb("hid", [P, 2, S])
        hid_hi = sb("hid_hi", [P, 3, S], F32R)
        hid_lo = sb("hid_lo", [P, 3, S], F32R)
        lo_squares = sb("lo_squares", [P, CHUNKS])
        lo_total = sb("lo_total", [P, 1])
        ones = sb("ffn_ones", [P, 1])
        lo_any = sb("lo_any", [1, 1], I32)

        down_ps = [pb(f"down_ps{t}") for t in range(TT)]
        gu_ps = [pb(f"gu_ps{n}") for n in range(3)]
        tr_ps = [pb(f"ffn_tr_ps{n}") for n in range(2)]

        consts_loaded = sem("ffn_consts_loaded")
        gate_ready = sem("ffn_gate_ready")
        gate_scaled = sem("ffn_gate_scaled")
        w_loaded = [sem(f"w_loaded{n}") for n in range(2)]
        w_float = sem("w_float")
        w_rounded = sem("w_rounded")
        w_split = sem("w_split")
        w_squared = sem("w_squared")
        lo_summed = sem("lo_summed")
        ones_ready = sem("ffn_ones_ready")
        lo_counted = sem("lo_counted")
        lo_flag = sem("lo_flag")
        half_ready = sem("ffn_half_ready")
        x2_loaded = [sem(f"x2_loaded{p}") for p in range(2)]
        stats_ready = sem("ffn_stats_ready")
        moments_ready = sem("ffn_moments_ready")
        var_ready = sem("ffn_var_ready")
        rstd_ready = sem("ffn_rstd_ready")
        xn_ready = sem("ffn_xn_ready")
        x_transposed = sem("ffn_x_transposed")
        x_rounded = sem("ffn_x_rounded")
        x_split = sem("ffn_x_split")
        gu_done = sem("gu_done")
        tanh_done = sem("tanh_done")
        silu_done = sem("silu_done")
        hid_done = sem("hid_done")
        hid_rounded = sem("hid_rounded")
        hid_split = sem("hid_split")
        down_step = sem("down_step")
        y_ready = sem("y_ready")
        y_stored = sem("y_stored")

        w_stage = [x2[:, n, :, :].rearrange("p t d -> p (t d)") for n in range(2)]
        w_f32 = xn[:, :, :].rearrange("p t d -> p (t d)")

        def chunk_of(tensor, n):
            return tensor[:, :, :].rearrange("p w c -> p (w c)")[:, n * CHUNK:(n + 1) * CHUNK]

        def chunk_source(n):
            w, at = divmod(n * CHUNK, COLS)
            if w < WD:
                src = (w_gate_t, w_up_t)[w].rearrange("p k h -> p (k h)")
            else:
                src = w_down_t.rearrange("p k d -> p (k d)")
            return src[:, at:at + CHUNK]

        block = ctx.enter_context(nc.Block())

        @block.sync
        def _(sp):
            sp.dma_start(identity[:, :], ident).then_inc(consts_loaded, 16)
            sp.dma_start(gate[:, :], g_ffn.to_broadcast([P, 1])).then_inc(consts_loaded, 16)
            for n in range(CHUNKS):
                if n >= 2:
                    sp.wait_ge(w_float, n - 1)
                sp.dma_start(w_stage[n % 2].bitcast(I32), chunk_source(n)).then_inc(w_loaded[n % 2], 16)

            def load(b):
                if b.exists:
                    sp.wait_ge(y_stored, (b + -1).count(16, 0))
                    sp.dma_start(x2[:, b.c, :, :], x2_dram[b.row].rearrange("(t p) d -> p t d", p=P)).then_inc(x2_loaded[b.c], 16)

            def store(b):
                sp.wait_ge(y_ready, b.count(TT, TT))
                sp.dma_start(out_dram[b.row].rearrange("(t p) d -> p t d", p=P), x2[:, b.c, :, :]).then_inc(y_stored, 16)

            sp.wait_ge(w_float, CHUNKS)
            load(Batch(0, 0))
            load(Batch(0, 1))

            def body(b):
                if (b + -1).exists:
                    store(b + -1)
                    load(b + 1)

            each_batch(sp, body)
            store(Batch(B // 2 - 1, 1))
            sp.wait_ge(y_stored, 16 * B)

        @block.gpsimd
        def _(pool):
            nc.gpsimd.memset(minus_half[:, :], -0.5).then_inc(half_ready, 1)
            pool.wait_ge(half_ready, 1)

            def inverse_std(b):
                if b.exists:
                    pool.wait_ge(xn_ready, b.count(TT, 0))
                    pool.wait_ge(var_ready, b.count(1, 1))
                    nc.gpsimd.tensor_tensor(rstd[:, :], var_eps[:, :], minus_half[:, :], ALU.pow).then_inc(rstd_ready, 1)

            inverse_std(Batch(0, 0))
            each_batch(pool, lambda b: inverse_std(b + 1))

        @block.scalar
        def _(act):
            act.wait_ge(consts_loaded, 32)
            nc.scalar.activation(gate[:, :], gate[:, :], ACT.Tanh).then_inc(gate_ready, 1)

            def round_x(b, u):
                if b.exists:
                    act.wait_ge(x_transposed, b.count(2, u + 1))
                    nc.scalar.activation(xt_hi[:, b.c, 2 * u:2 * u + 2, :], tr_ps[u][:, :].rearrange("p (k s) -> p k s", k=2),
                                         ACT.Copy).then_inc(x_rounded, 1)

            def tanh(b, k):
                act.wait_ge(silu_done, b.count(HT, k - 1))
                act.wait_ge(gu_done, b.count(HT, k + 1))
                nc.scalar.activation(th[:, k % 2, :], gu_ps[k % 3][:, 0:S], ACT.Tanh, scale=0.5 * DEQ).then_inc(tanh_done, 1)

            def round_hidden(b, k):
                act.wait_ge(down_step, b.count(HT, k - 2))
                act.wait_ge(hid_done, b.count(HT, k + 1))
                nc.scalar.activation(hid_hi[:, k % 3, :], hid[:, k % 2, :], ACT.Copy).then_inc(hid_rounded, 1)

            for u in range(2):
                round_x(Batch(0, 0), u)

            def body(b):
                for k in range(HT):
                    tanh(b, k)
                    if k:
                        round_hidden(b, k - 1)
                    elif (b + -1).exists:
                        round_hidden(b + -1, HT - 1)
                    if k in (7, 9):
                        round_x(b + 1, (k - 7) // 2)

            each_batch(act, body)
            round_hidden(Batch(B // 2 - 1, 1), HT - 1)

        @block.vector
        def _(dve):
            dve.wait_ge(gate_ready, 1)
            nc.vector.tensor_scalar(gate[:, :], gate[:, :], DEQ, None, ALU.mult).then_inc(gate_scaled, 1)
            nc.vector.memset(ones[:, :], 1.0).then_inc(ones_ready, 1)
            for n in range(CHUNKS):
                dve.wait_ge(w_loaded[n % 2], 16 * (n // 2 + 1))
                if n:
                    dve.wait_ge(w_split, n)
                nc.vector.tensor_copy(w_f32, w_stage[n % 2].bitcast(I32)).then_inc(w_float, 1)
                dve.wait_ge(w_float, n + 1)
                nc.vector.tensor_copy(chunk_of(w_hi, n), w_f32).then_inc(w_rounded, 1)
                dve.wait_ge(w_rounded, n + 1)
                nc.vector.tensor_tensor(chunk_of(w_lo, n), w_f32, chunk_of(w_hi, n).bitcast(F32), ALU.subtract).then_inc(w_split, 1)
                dve.wait_ge(w_split, n + 1)
                nc.vector.tensor_tensor_reduce(out=w_f32, in0=chunk_of(w_lo, n).bitcast(F32), in1=chunk_of(w_lo, n).bitcast(F32),
                                               scale=1.0, scalar=0.0, op0=ALU.mult, op1=ALU.add,
                                               accum_out=lo_squares[:, n:n + 1]).then_inc(w_squared, 1)
                dve.wait_ge(w_squared, n + 1)
            nc.vector.reduce_sum(lo_total[:, :], lo_squares[:, :], axis=AX.X).then_inc(lo_summed, 1)
            dve.wait_ge(lo_counted, 1)
            nc.vector.tensor_scalar(lo_any[:, :], down_ps[0][0:1, 0:1], 0.0, None, ALU.is_gt).then_inc(lo_flag, 1)
            dve.wait_ge(gate_scaled, 1)

            def statistics(b):
                if b.exists:
                    dve.wait_ge(x2_loaded[b.c], b.half_count(16))
                    for t in range(TT):
                        last = nc.vector.bn_stats(stats[:, t, :], x2[:, b.c, t, :])
                    last.then_inc(stats_ready, 1)

            def statistics_there(b):
                if b.exists:
                    dve.wait_ge(stats_ready, b.count(1, 1))

            def aggregate(b):
                if b.exists:
                    for t in range(TT):
                        last = nc.vector.bn_aggr(moments[:, t, :], stats[:, t, :])
                    last.then_inc(moments_ready, 1)

            def variance(b):
                if b.exists:
                    dve.wait_ge(moments_ready, b.count(1, 1))
                    nc.vector.tensor_scalar(var_eps[:, :], moments[:, :, 1], EPS, None, ALU.add).then_inc(var_ready, 1)

            def normalise(b, t):
                if b.exists:
                    dve.wait_ge(x_transposed, b.count(2, 0))
                    dve.wait_ge(rstd_ready, b.count(1, 1))
                    nc.vector.tensor_scalar(xn[:, t, :], x2[:, b.c, t, :], moments[:, t, 0:1], rstd[:, t:t + 1],
                                            ALU.subtract, ALU.mult).then_inc(xn_ready, 1)

            def split_x(b, u):
                if b.exists:
                    dve.wait_ge(x_rounded, b.count(2, u + 1))
                    nc.vector.tensor_tensor(xt_lo[:, b.c, 2 * u:2 * u + 2, :], tr_ps[u][:, :].rearrange("p (k s) -> p k s", k=2),
                                            xt_hi[:, b.c, 2 * u:2 * u + 2, :].bitcast(F32), ALU.subtract).then_inc(x_split, 1)

            def silu(b, k):
                dve.wait_ge(tanh_done, b.count(HT, k + 1))
                nc.vector.scalar_tensor_tensor(silu2[:, k % 2, :], th[:, k % 2, :], 1.0, gu_ps[k % 3][:, 0:S],
                                               ALU.add, ALU.mult).then_inc(silu_done, 1)

            def hidden(b, k):
                dve.wait_ge(hid_rounded, b.count(HT, k - 1))
                dve.wait_ge(silu_done, b.count(HT, k + 1))
                nc.vector.scalar_tensor_tensor(hid[:, k % 2, :], silu2[:, k % 2, :], 0.5 * DEQ * DEQ, gu_ps[k % 3][:, S:2 * S],
                                               ALU.mult, ALU.mult).then_inc(hid_done, 1)

            def split_hidden(b, k):
                dve.wait_ge(down_step, b.count(HT, k - 2))
                dve.wait_ge(hid_rounded, b.count(HT, k + 1))
                nc.vector.tensor_tensor(hid_lo[:, k % 3, :], hid[:, k % 2, :], hid_hi[:, k % 3, :].bitcast(F32),
                                        ALU.subtract).then_inc(hid_split, 1)

            def output(b, t):
                dve.wait_ge(down_step, b.count(HT, HT))
                nc.vector.scalar_tensor_tensor(x2[:, b.c, t, :], down_ps[t][:, :], gate[:, 0:1], x2[:, b.c, t, :],
                                               ALU.mult, ALU.add).then_inc(y_ready, 1)

            first = Batch(0, 0)
            statistics(first)
            statistics_there(first)
            aggregate(first)
            variance(first)
            for t in range(TT):
                normalise(first, t)
            for u in range(2):
                split_x(first, u)

            def body(b):
                for k in range(HT):
                    if k == 4:
                        statistics_there(b + 1)
                    silu(b, k)
                    if k:
                        split_hidden(b, k - 1)
                    elif (b + -1).exists:
                        split_hidden(b + -1, HT - 1)
                    hidden(b, k)
                    if k == 2 and (b + -1).exists:
                        for t in range(TT):
                            output(b + -1, t)
                    if k == 3:
                        statistics(b + 1)
                    if k == 4:
                        aggregate(b + 1)
                        variance(b + 1)
                    if k in (5, 6):
                        normalise(b + 1, k - 5)
                    if k in (7, 9):
                        split_x(b + 1, (k - 7) // 2)

            each_batch(dve, body)
            last = Batch(B // 2 - 1, 1)
            split_hidden(last, HT - 1)
            for t in range(TT):
                output(last, t)

        @block.tensor
        def _(pe):
            pe.wait_ge(ones_ready, 1)
            pe.wait_ge(lo_summed, 1)
            nc.tensor.matmul(down_ps[0][0:1, 0:1], lo_total[:, :], ones[:, :], start=True, stop=True).then_inc(lo_counted, 1)
            pe.wait_ge(lo_flag, 1)
            any_lo = pe.value_load(lo_any[0:1, 0:1], min_val=0, max_val=1)

            def gate_up(b, k):
                pe.wait_ge(hid_done, b.count(HT, k - 2))
                if k == 0:
                    pe.wait_ge(x_split, b.count(2, 2))
                for w in (WG, WU):
                    out = gu_ps[k % 3][:, w * S:(w + 1) * S]

                    def cols(weights, i):
                        return weights[:, w, i * HID + k * P:i * HID + (k + 1) * P]

                    for i in range(KT):
                        nc.tensor.matmul(out, cols(w_hi, i), xt_hi[:, b.c, i, :], start=(i == 0), stop=False)
                    with pe.If(any_lo > 0):
                        for i in range(KT):
                            nc.tensor.matmul(out, cols(w_lo, i), xt_hi[:, b.c, i, :], start=False, stop=False)
                    for i in range(KT):
                        last = nc.tensor.matmul(out, cols(w_hi, i), xt_lo[:, b.c, i, :], start=False, stop=(i == KT - 1))
                last.then_inc(gu_done, 1)

            def down(b, k):
                pe.wait_ge(hid_split, b.count(HT, k + 1))
                if k == 0:
                    pe.wait_ge(y_ready, b.count(TT, 0))
                for t in range(TT):
                    tok = slice(t * P, (t + 1) * P)

                    def cols(weights):
                        return weights[:, WD, k * D:(k + 1) * D]

                    nc.tensor.matmul(down_ps[t][:, :], hid_hi[:, k % 3, tok], cols(w_hi), start=(k == 0), stop=False)
                    with pe.If(any_lo > 0):
                        nc.tensor.matmul(down_ps[t][:, :], hid_hi[:, k % 3, tok], cols(w_lo), start=False, stop=False)
                    last = nc.tensor.matmul(down_ps[t][:, :], hid_lo[:, k % 3, tok], cols(w_hi), start=False, stop=(k == HT - 1))
                last.then_inc(down_step, 1)

            def transpose(b, u):
                if b.exists:
                    pe.wait_ge(xn_ready, b.count(TT, TT))
                    pe.wait_ge(x_split, b.count(2, u - 1))
                    for k in range(2):
                        for t in range(TT):
                            at = (k * TT + t) * P
                            last = nc.tensor.transpose(tr_ps[u][:, at:at + P], xn[:, t, (2 * u + k) * P:(2 * u + k + 1) * P],
                                                       identity[:, :])
                    last.then_inc(x_transposed, 1)

            for u in range(2):
                transpose(Batch(0, 0), u)

            def body(b):
                for k in range(HT):
                    gate_up(b, k)
                    if k >= 2:
                        down(b, k - 2)
                    elif (b + -1).exists:
                        down(b + -1, HT - 2 + k)
                    if k in (7, 9):
                        transpose(b + 1, (k - 7) // 2)

            each_batch(pe, body)
            for k in (HT - 2, HT - 1):
                down(Batch(B // 2 - 1, 1), k)


def tables():
    theta = (1.0 / np.float32(ROPE_BASE) ** (np.arange(0, DH, 2, dtype=np.float32) / np.float32(DH))).astype(np.float32)
    angle = np.arange(S, dtype=np.float32)[:, None] * theta[None, :]
    cos = np.repeat(np.cos(angle), 2, axis=1).astype(np.float32)
    sin = np.stack([-np.sin(angle), np.sin(angle)], axis=2).reshape(S, DH).astype(np.float32)
    by_tile = lambda a: np.ascontiguousarray(a.reshape(TT, P, DH).transpose(1, 0, 2))
    seen = np.tril(np.ones((S, S), bool))
    causal = np.where(np.concatenate([seen[0:P, 0:P], seen[P:S, :]], axis=1), 0.0, -BIG).astype(np.float32)
    return {"cos": by_tile(cos), "sin": by_tile(sin), "causal": causal, "ident": np.eye(P, dtype=np.float32)}


def kernel(x, ctx_1024, mask_BxS2_if1, g_xattn, g_ffn, L0_xattn_Wq, L0_xattn_Wk, L0_xattn_Wv, L0_xattn_Wo, L0_xattn_bo,
           L0_ffn_w_gate, L0_ffn_w_up, L0_ffn_w_down):
    import concourse.bacc as bacc
    from concourse.bass_utils import run_bass_kernel_spmd

    def c(a):
        return np.ascontiguousarray(a)

    def tiled(w_t):
        w_t = np.asarray(w_t)
        return c(w_t.reshape(-1, P, w_t.shape[1]).transpose(1, 0, 2))

    arrays = {
        "x": c(x), "ctx_t": c(np.asarray(ctx_1024).transpose(0, 2, 1)), "mask": c(mask_BxS2_if1),
        "g_xattn": c(np.asarray(g_xattn).reshape(1, 1)), "g_ffn": c(np.asarray(g_ffn).reshape(1, 1)),
        "wq_t": c(np.asarray(L0_xattn_Wq).T), "wk_t": c(np.asarray(L0_xattn_Wk).T),
        "wv_t": c(np.asarray(L0_xattn_Wv).T), "wo_t": c(np.asarray(L0_xattn_Wo).T),
        "bo": c(np.asarray(L0_xattn_bo).reshape(1, D)),
        "w_gate_t": tiled(np.asarray(L0_ffn_w_gate).T), "w_up_t": tiled(np.asarray(L0_ffn_w_up).T),
        "w_down_t": tiled(np.asarray(L0_ffn_w_down).T),
        **tables(),
    }
    nc = bacc.Bacc("TRN2", target_bir_lowering=False, num_devices=1)
    d = {n: nc.dram_tensor(f"in_{n}", a.shape, mybir.dt.from_np(a.dtype), kind="ExternalInput").ap() for n, a in arrays.items()}
    x2_dram = nc.dram_tensor("x2_scratch", (B, S, D), F32, kind="Internal").ap()
    out = nc.dram_tensor("out_y", (B, S, D), F32, kind="ExternalOutput").ap()
    attention_phase(nc, d["x"], d["ctx_t"], d["mask"], d["g_xattn"], d["wq_t"], d["wk_t"], d["wv_t"], d["wo_t"], d["bo"],
                    d["cos"], d["sin"], d["causal"], d["ident"], x2_dram)
    ffn_phase(nc, x2_dram, d["g_ffn"], d["w_gate_t"], d["w_up_t"], d["w_down_t"], d["ident"], out)
    r = run_bass_kernel_spmd(nc, [{f"in_{n}": a for n, a in arrays.items()}], core_ids=[0])
    return r.results[0]["out_y"]
```

```python
import math
from contextlib import ExitStack

import numpy as np

import concourse.bass as bass
from concourse import mybir

F32 = mybir.dt.float32
F32R = mybir.dt.float32r
I32 = mybir.dt.int32
ALU = mybir.AluOpType
ACT = mybir.ActivationFunctionType
AX = mybir.AxisListType

P = 128
B, S, D = 32, 256, 512
H, DH = 16, 32
HID = 1536
TT = S // P
KT = D // P
HG = P // DH
HT = HID // P
EPS = 1e-5
SCALE = 1.0 / math.sqrt(DH)
DEQ = float(np.float32(1.0 / 127.0))
STACK = 3 * DH
STACK_DMAS = 3 * HG
ROPE_BASE = 10000.0
BIG = 1.0e30


class Batch:

    def __init__(self, j, c):
        self.j, self.c = j, c

    def __add__(self, d):
        return Batch(self.j + (self.c + d) // 2 if (self.c + d) // 2 else self.j, (self.c + d) % 2)

    @property
    def row(self):
        return self.j * 2 + self.c

    @property
    def exists(self):
        return not isinstance(self.j, int) or 0 <= self.row < B

    def head(self, h):
        return self + h // H, h % H

    def count(self, per_row, n):
        value = self.row * per_row + n
        return max(value, 0) if isinstance(value, int) else value

    def half_count(self, n):
        return self.j * n + n


def each_batch(eng, body):
    for c in range(2):
        body(Batch(0, c))
    with eng.Fori(1, B // 2 - 1) as j:
        for c in range(2):
            body(Batch(j, c))
    for c in range(2):
        body(Batch(B // 2 - 1, c))


def attention_phase(nc, x, ctx_t, mask, g_xattn, wq_t, wk_t, wv_t, wo_t, bo, cos, sin, causal, ident, x2_dram):
    with ExitStack() as ctx:
        def sb(name, shape, dt=F32):
            return ctx.enter_context(nc.sbuf_tensor(name, shape, dt))

        def pb(name):
            return ctx.enter_context(nc.psum_tensor(name, [P, 512], F32))

        def sem(name):
            return ctx.enter_context(nc.semaphore(name))

        weights = {"k": wk_t, "q": wq_t, "v": wv_t, "o": wo_t}
        w_hi = {n: sb(f"w{n}_hi", [P, KT, D], F32R) for n in weights}
        w_lo = {n: sb(f"w{n}_lo", [P, KT, D], F32R) for n in weights}
        identity = sb("identity", [P, P])
        cos_sb = sb("cos_sb", [P, TT, DH])
        sin_sb = sb("sin_sb", [P, TT, DH])
        causal_sb = sb("causal_sb", [P, 3 * P])
        gate = sb("gate", [P, 1])
        gate_bo = sb("gate_bo", [P, D])
        x_raw = sb("x_raw", [P, TT, D])
        res_room = sb("res_room", [P, 2, TT, D])
        x_res = res_room[:, 0, :, :]
        xnt_hi = sb("xnt_hi", [P, KT, S], F32R)
        xnt_lo = sb("xnt_lo", [P, KT, S], F32R)
        ctx_raw = sb("ctx_raw", [P, KT, S])
        ctx_hi = sb("ctx_hi", [P, KT, S], F32R)
        ctx_lo = sb("ctx_lo", [P, KT, S], F32R)
        stats = sb("stats", [P, TT, 6])
        moments = sb("moments", [P, TT, 2])
        var_eps = sb("var_eps", [P, TT])
        rstd = sb("rstd", [P, TT])
        neg_mean = sb("neg_mean", [P, TT])
        shift = sb("shift", [P, TT])
        minus_half = sb("minus_half", [P, TT])
        roped = {n: sb(f"{n}_roped", [P, TT, D]) for n in "qk"}
        xn = roped["q"]
        rope_sin = sb("rope_sin", [P, D])
        qt_hi = sb("qt_hi", [P, KT, S], F32R)
        qt_lo = sb("qt_lo", [P, KT, S], F32R)
        kt_hi = sb("kt_hi", [P, KT, S], F32R)
        kt_lo = sb("kt_lo", [P, KT, S], F32R)
        q_stack = sb("q_stack", [STACK, H, S], F32R)
        k_stack = sb("k_stack", [STACK, 2, H, S], F32R)
        v_sb = sb("v_sb", [P, 2, TT, D])
        w_stage = [room[:, :, :, :].rearrange("p a b n -> p (a b) n") for room in (v_sb, res_room)]
        mask_int = sb("mask_int", [P, S], I32)
        pad = sb("pad", [P, S])
        mask_sb = sb("mask_sb", [P, 2, 3 * P])
        prob = sb("prob", [P, 4, 3 * P])
        neg_max = sb("neg_max", [P, 4, TT])
        row_sum = sb("row_sum", [P, 4, TT])
        row_rcp = sb("row_rcp", [P, 4, TT])
        probt = sb("probt", [P, 2, 3 * P])
        ot_hi = sb("ot_hi", [P, KT, S], F32R)
        ot_lo = sb("ot_lo", [P, KT, S], F32R)

        proj_ps = [pb(f"proj_ps{t}") for t in range(TT)]
        tr_ps = pb("tr_ps")
        score_ps = [pb(f"score_ps{n}") for n in range(2)]
        probt_ps = pb("probt_ps")
        out_ps = [pb(f"out_ps{n}") for n in range(2)]

        consts_loaded = sem("consts_loaded")
        weight_loaded = [sem(f"w{n}_loaded") for n in weights]
        weight_rounded = sem("weight_rounded")
        weight_split = sem("weight_split")
        gate_ready = sem("gate_ready")
        gate_bo_ready = sem("gate_bo_ready")
        half_ready = sem("half_ready")
        x_loaded = sem("x_loaded")
        ctx_loaded = sem("ctx_loaded")
        mask_loaded = sem("mask_loaded")
        ctx_rounded = sem("ctx_rounded")
        ctx_split = sem("ctx_split")
        res_loaded = sem("res_loaded")
        res_ready = sem("res_ready")
        stats_ready = sem("stats_ready")
        moments_ready = sem("moments_ready")
        var_ready = sem("var_ready")
        rstd_ready = sem("rstd_ready")
        shift_ready = sem("shift_ready")
        xn_ready = sem("xn_ready")
        pad_ready = sem("pad_ready")
        mask_ready = sem("mask_ready")
        projected = {n: sem(f"{n}_projected") for n in "qkvo"}
        transposed = {n: sem(f"{n}_transposed") for n in "xqk"}
        rounded = {n: sem(f"{n}_rounded") for n in "xqk"}
        split = {n: sem(f"{n}_split") for n in "xqk"}
        rope_read = {n: sem(f"{n}_rope_read") for n in "qk"}
        rope_added = {n: sem(f"{n}_rope_added") for n in "qk"}
        k_stacked = sem("k_stacked")
        q_stacked = [sem(f"q_stacked{u}") for u in range(2)]
        v_copied = sem("v_copied")
        scored = sem("scored")
        masked = sem("masked")
        exp_done = sem("exp_done")
        rcp_done = sem("rcp_done")
        normed = sem("normed")
        prob_transposed = sem("prob_transposed")
        probt_copied = sem("probt_copied")
        pv_done = sem("pv_done")
        out_rounded = sem("out_rounded")
        out_split = sem("out_split")
        out_half_read = sem("out_half_read")
        x2_ready = sem("x2_ready")
        x2_stored = sem("x2_stored")

        CONSTS = 6
        block = ctx.enter_context(nc.Block())

        @block.sync
        def _(sp):
            for dst, src in ((identity, ident), (cos_sb, cos), (sin_sb, sin), (causal_sb, causal)):
                sp.dma_start(dst[:], src).then_inc(consts_loaded, 16)
            sp.dma_start(gate[:, :], g_xattn.to_broadcast([P, 1])).then_inc(consts_loaded, 16)
            sp.dma_start(gate_bo[:, :], bo.to_broadcast([P, D])).then_inc(consts_loaded, 16)

            def load_weight(n):
                if n >= 2:
                    sp.wait_ge(weight_split, n - 1)
                sp.dma_start(w_stage[n % 2], list(weights.values())[n].rearrange("(k p) n -> p k n", p=P)).then_inc(weight_loaded[n], 16)

            def load_x(b):
                if b.exists:
                    tokens = x[b.row].rearrange("(t p) d -> p t d", p=P)
                    sp.wait_ge(xn_ready, b.count(TT, 0))
                    sp.dma_start(x_raw[:, :, :], tokens).then_inc(x_loaded, 16)

            def load_residual(b):
                if b.exists:
                    tokens = x[b.row].rearrange("(t p) d -> p t d", p=P)
                    sp.wait_ge(x2_stored, b.count(16, 0))
                    sp.dma_start(x_res[:, :, :], tokens).then_inc(res_loaded, 16)

            def load_ctx(b):
                if b.exists:
                    features = ctx_t[b.row].rearrange("(k p) s -> p k s", p=P)
                    sp.wait_ge(ctx_split, b.count(1, 0))
                    sp.dma_start(ctx_raw[:, :, :], features).then_inc(ctx_loaded, 16)

            def load_mask(b):
                if b.exists:
                    keys = mask[bass.ds(b.row, 1), :].to_broadcast([P, S])
                    sp.wait_ge(pad_ready, b.count(1, 0))
                    sp.dma_start(mask_int[:, :], keys).then_inc(mask_loaded, 16)

            def stack_k(b):
                if b.exists:
                    sp.wait_ge(split["k"], b.count(2, 2))
                    dst = k_stack[:, b.c, :, :].rearrange("r (t q) s -> r t q s", q=HG)
                    for block_no, src in enumerate((kt_hi, kt_lo, kt_hi)):
                        for q in range(HG):
                            sp.dma_start(dst[block_no * DH:(block_no + 1) * DH, :, q, :].bitcast(F32),
                                         src[q * DH:(q + 1) * DH, :, :].bitcast(F32)).then_inc(k_stacked, 16)

            def stack_q(b, u):
                if b.exists:
                    if u == 0:
                        sp.wait_ge(split["q"], b.count(2, 2))
                    else:
                        sp.wait_ge(scored, b.count(H, 0))
                    dst = q_stack[:, :, :].rearrange("r (t q) s -> r t q s", q=HG)
                    for block_no, src in enumerate((qt_hi, qt_hi, qt_lo)):
                        for q in range(HG):
                            sp.dma_start(dst[block_no * DH:(block_no + 1) * DH, 2 * u:2 * u + 2, q, :].bitcast(F32),
                                         src[q * DH:(q + 1) * DH, 2 * u:2 * u + 2, :].bitcast(F32)).then_inc(q_stacked[u], 16)

            def store_x2(b):
                if b.exists:
                    tokens = x2_dram[b.row].rearrange("(t p) d -> p t d", p=P)
                    sp.wait_ge(x2_ready, b.count(TT, TT))
                    sp.dma_start(tokens, x_res[:, :, :]).then_inc(x2_stored, 16)

            def body(b):
                load_x(b + 2)
                load_ctx(b + 2)
                load_residual(b + -1)
                stack_q(b, 1)
                load_mask(b + 2)
                stack_k(b + 1)
                stack_q(b + 1, 0)
                store_x2(b + -1)

            for n in range(2):
                load_weight(n)
            body(Batch(-1, 0))
            for n in range(2, 4):
                load_weight(n)
            body(Batch(-1, 1))
            each_batch(sp, body)
            body(Batch(B // 2, 0))
            sp.wait_ge(x2_stored, 16 * B)

        @block.gpsimd
        def _(pool):
            nc.gpsimd.memset(minus_half[:, :], -0.5).then_inc(half_ready, 1)
            pool.wait_ge(half_ready, 1)

            def split_ctx(b):
                if b.exists:
                    pool.wait_ge(projected["v"], b.count(TT, 0))
                    pool.wait_ge(ctx_rounded, b.count(1, 1))
                    nc.gpsimd.tensor_tensor(ctx_lo[:, :, :], ctx_raw[:, :, :], ctx_hi[:, :, :].bitcast(F32),
                                            ALU.subtract).then_inc(ctx_split, 1)

            def inverse_std(b):
                if b.exists:
                    pool.wait_ge(xn_ready, b.count(TT, 0))
                    pool.wait_ge(var_ready, b.count(1, 1))
                    nc.gpsimd.tensor_tensor(rstd[:, :], var_eps[:, :], minus_half[:, :], ALU.pow).then_inc(rstd_ready, 1)
                    pool.wait_ge(rstd_ready, b.count(1, 1))
                    nc.gpsimd.tensor_tensor(shift[:, :], neg_mean[:, :], rstd[:, :], ALU.mult).then_inc(shift_ready, 1)

            def rope_add(name, b, t):
                if b.exists:
                    pool.wait_ge(rope_read[name], b.count(TT, t + 1))
                    nc.gpsimd.tensor_tensor(roped[name][:, t, :], roped[name][:, t, :], rope_sin[:, :],
                                            ALU.add).then_inc(rope_added[name], 1)

            def residual(b):
                if b.exists:
                    pool.wait_ge(gate_bo_ready, 2)
                    pool.wait_ge(res_loaded, b.count(16, 16))
                    nc.gpsimd.tensor_tensor(x_res[:, :, :], x_res[:, :, :], gate_bo[:, :].unsqueeze(1).to_broadcast([P, TT, D]),
                                            ALU.add).then_inc(res_ready, 1)

            def body(b):
                rope_add("k", b + 1, 1)
                for t in range(TT):
                    rope_add("q", b + 1, t)
                residual(b + -1)
                inverse_std(b + 2)
                split_ctx(b + 2)
                rope_add("k", b + 2, 0)

            for c in range(2):
                body(Batch(-1, c))
            each_batch(pool, body)
            body(Batch(B // 2, 0))

        @block.scalar
        def _(act):
            act.wait_ge(consts_loaded, 16 * CONSTS)
            nc.scalar.activation(gate[:, :], gate[:, :], ACT.Tanh).then_inc(gate_ready, 1)

            def round_weight(n, name):
                act.wait_ge(weight_loaded[n], 16)
                nc.scalar.activation(w_hi[name][:, :, :], w_stage[n % 2],
                                     ACT.Copy).then_inc(weight_rounded, 1)

            def exponentials(b, h):
                if not b.exists:
                    return
                n = h % 4
                act.wait_ge(masked, b.count(H, h + 1))
                for t, (lo, hi) in enumerate(((0, P), (P, 3 * P))):
                    last = nc.scalar.activation(prob[:, n, lo:hi], prob[:, n, lo:hi], ACT.Exp, bias=neg_max[:, n, t:t + 1],
                                                scale=-1.0, accum_out=row_sum[:, n, t:t + 1])
                last.then_inc(exp_done, 1)

            def copy_probt(b, h):
                if not b.exists:
                    return
                act.wait_ge(pv_done, b.count(H, h - 1))
                act.wait_ge(prob_transposed, b.count(H, h + 1))
                nc.scalar.activation(probt[:, h % 2, :], probt_ps[:, 0:3 * P], ACT.Copy).then_inc(probt_copied, 1)

            def round_transposed(name, b, u, dst):
                if b.exists:
                    if name == "x":
                        act.wait_ge(projected["q"], b.count(TT, 0))
                    elif name == "k":
                        act.wait_ge(k_stacked, b.count(16 * STACK_DMAS, 0))
                    else:
                        act.wait_ge(q_stacked[u], b.count(16 * STACK_DMAS, 0))
                    act.wait_ge(transposed[name], b.count(2, u + 1))
                    nc.scalar.activation(dst[:, 2 * u:2 * u + 2, :], tr_ps[:, :].rearrange("p (k s) -> p k s", k=2),
                                         ACT.Copy).then_inc(rounded[name], 1)

            def copy_v(b, t):
                if b.exists:
                    act.wait_ge(pv_done, b.count(H, -H))
                    act.wait_ge(projected["v"], b.count(TT, t + 1))
                    nc.scalar.activation(v_sb[:, b.c, t, :], proj_ps[t][:, :], ACT.Copy).then_inc(v_copied, 1)

            def round_out(b, g):
                if not b.exists:
                    return
                if g < 2:
                    act.wait_ge(out_half_read, b.count(1, 0))
                else:
                    act.wait_ge(projected["o"], b.count(TT, 0))
                act.wait_ge(pv_done, b.count(H, HG * g + HG))
                nc.scalar.activation(ot_hi[:, g, :], out_ps[g % 2][:, 0:S], ACT.Copy).then_inc(out_rounded, 1)

            def normalise(b, t):
                if b.exists:
                    act.wait_ge(transposed["q"], b.count(2, 0))
                    act.wait_ge(shift_ready, b.count(1, 1))
                    nc.scalar.activation(xn[:, t, :], x_raw[:, t, :], ACT.Identity, bias=shift[:, t:t + 1],
                                         scale=rstd[:, t:t + 1]).then_inc(xn_ready, 1)

            def body(b):
                for s in range(H):
                    copy_probt(*b.head(s - 4))
                    exponentials(b, s)
                    if s in (3, 5):
                        round_transposed("k", b + 1, (s - 3) // 2, kt_hi)
                    if s in (7, 9):
                        round_transposed("q", b + 1, (s - 7) // 2, qt_hi)
                    if s in (6, 8):
                        copy_v(b + 1, (s - 6) // 2)
                    if s in (12, 14):
                        round_transposed("x", b + 2, (s - 12) // 2, xnt_hi)
                    if s == 10:
                        for t in range(TT):
                            normalise(b + 2, t)
                    if s in (1, 5):
                        round_out(b + -1, 2 + s // 4)
                    if s in (11, 13):
                        round_out(b, (s - 11) // 2)

            names = list(weights)
            for n in range(2):
                round_weight(n, names[n])
            body(Batch(-1, 0))
            for n in range(2, 4):
                round_weight(n, names[n])
            body(Batch(-1, 1))
            each_batch(act, body)
            body(Batch(B // 2, 0))

        @block.vector
        def _(dve):
            dve.wait_ge(gate_ready, 1)
            nc.vector.tensor_scalar(gate_bo[:, :], gate_bo[:, :], gate[:, 0:1], None, ALU.mult).then_inc(gate_bo_ready, 2)

            def split_weight(n, name):
                dve.wait_ge(weight_rounded, n + 1)
                nc.vector.tensor_tensor(w_lo[name][:, :, :], w_stage[n % 2],
                                        w_hi[name][:, :, :].bitcast(F32), ALU.subtract).then_inc(weight_split, 1)

            def statistics(b):
                if b.exists:
                    dve.wait_ge(x_loaded, b.count(16, 16))
                    for t in range(TT):
                        last = nc.vector.bn_stats(stats[:, t, :], x_raw[:, t, :])
                    last.then_inc(stats_ready, 1)

            def statistics_there(b):
                if b.exists:
                    dve.wait_ge(stats_ready, b.count(1, 1))

            def variance(b):
                if b.exists:
                    for t in range(TT):
                        last = nc.vector.bn_aggr(moments[:, t, :], stats[:, t, :])
                    last.then_inc(moments_ready, 1)
                    dve.wait_ge(xn_ready, b.count(TT, 0))
                    dve.wait_ge(moments_ready, b.count(1, 1))
                    nc.vector.tensor_scalar(neg_mean[:, :], moments[:, :, 0], -1.0, None, ALU.mult)
                    nc.vector.tensor_scalar(var_eps[:, :], moments[:, :, 1], EPS, None, ALU.add).then_inc(var_ready, 1)

            def split_transposed(name, b, u, hi, lo):
                if b.exists:
                    dve.wait_ge(rounded[name], b.count(2, u + 1))
                    nc.vector.tensor_tensor(lo[:, 2 * u:2 * u + 2, :], tr_ps[:, :].rearrange("p (k s) -> p k s", k=2),
                                            hi[:, 2 * u:2 * u + 2, :].bitcast(F32), ALU.subtract).then_inc(split[name], 1)

            def rope(name, b, t):
                if b.exists:
                    if t:
                        dve.wait_ge(rope_added[name], b.count(TT, t))
                    elif name == "q":
                        dve.wait_ge(rope_added["k"], b.count(TT, TT))
                    else:
                        dve.wait_ge(rope_added["q"], b.count(TT, 0))
                    dve.wait_ge(transposed[name], b.count(2, 0))
                    dve.wait_ge(projected[name], b.count(TT, t + 1))
                    table = cos_sb[:, t, :].unsqueeze(1).to_broadcast([P, H, DH])
                    nc.vector.tensor_tensor(roped[name][:, t, :].rearrange("p (h d) -> p h d", h=H),
                                            proj_ps[t][:, :].rearrange("p (h d) -> p h d", h=H), table, ALU.mult)
                    for e in range(2):
                        pairs = proj_ps[t][:, :].rearrange("p (h i e) -> p h i e", h=H, e=2)
                        signs = sin_sb[:, t, :].rearrange("p (i e) -> p i e", e=2)[:, :, e].unsqueeze(1).to_broadcast([P, H, DH // 2])
                        last = nc.vector.tensor_tensor(rope_sin[:, :].rearrange("p (h i e) -> p h i e", h=H, e=2)[:, :, :, e],
                                                       pairs[:, :, :, 1 - e], signs, ALU.mult)
                    last.then_inc(rope_read[name], 1)

            def round_ctx(b):
                if b.exists:
                    dve.wait_ge(projected["v"], b.count(TT, 0))
                    dve.wait_ge(ctx_loaded, b.count(16, 16))
                    nc.vector.tensor_copy(ctx_hi[:, :, :], ctx_raw[:, :, :]).then_inc(ctx_rounded, 1)

            def padding(b):
                if b.exists:
                    dve.wait_ge(mask_loaded, b.count(16, 16))
                    nc.vector.tensor_scalar(pad[:, :], mask_int[:, :], 0.0, -BIG, ALU.is_equal, ALU.mult).then_inc(pad_ready, 1)

            def build_mask(b):
                if b.exists:
                    dve.wait_ge(pad_ready, b.count(1, 1))
                    for lo, hi in ((0, P), (P, 3 * P)):
                        last = nc.vector.scalar_tensor_tensor(mask_sb[:, b.c, lo:hi], pad[:, 0:hi - lo], 1.0,
                                                              causal_sb[:, lo:hi], ALU.mult, ALU.add)
                    last.then_inc(mask_ready, 1)

            def scores_there(b, h):
                if not b.exists:
                    return
                dve.wait_ge(prob_transposed, b.count(H, h - 3))
                dve.wait_ge(scored, b.count(H, h + 1))

            def mask_scores(b, h):
                if not b.exists:
                    return
                n = h % 4
                for t, (lo, hi) in enumerate(((0, P), (P, 3 * P))):
                    last = nc.vector.tensor_tensor_reduce(out=prob[:, n, lo:hi], in0=score_ps[h % 2][:, lo:hi],
                                                          in1=mask_sb[:, b.c, lo:hi], scale=-SCALE, scalar=3.0e38, op0=ALU.add,
                                                          op1=ALU.min, accum_out=neg_max[:, n, t:t + 1])
                last.then_inc(masked, 1)

            def reciprocal_sum(b, h):
                if not b.exists:
                    return
                dve.wait_ge(exp_done, b.count(H, h + 1))
                nc.vector.reciprocal(row_rcp[:, h % 4, :], row_sum[:, h % 4, :]).then_inc(rcp_done, 1)

            def normalise_probs(b, h):
                if not b.exists:
                    return
                n = h % 4
                dve.wait_ge(rcp_done, b.count(H, h + 1))
                for t, (lo, hi) in enumerate(((0, P), (P, 3 * P))):
                    last = nc.vector.tensor_scalar(prob[:, n, lo:hi], prob[:, n, lo:hi], row_rcp[:, n, t:t + 1], None, ALU.mult)
                last.then_inc(normed, 1)

            def split_out(b, g):
                if not b.exists:
                    return
                dve.wait_ge(out_rounded, b.count(KT, g + 1))
                nc.vector.tensor_tensor(ot_lo[:, g, :], out_ps[g % 2][:, 0:S], ot_hi[:, g, :].bitcast(F32),
                                        ALU.subtract).then_inc(out_split, 1)

            def add_residual(b, t):
                if not b.exists:
                    return
                dve.wait_ge(res_ready, b.count(1, 1))
                dve.wait_ge(projected["o"], b.count(TT, t + 1))
                nc.vector.scalar_tensor_tensor(x_res[:, t, :], proj_ps[t][:, :], gate[:, 0:1], x_res[:, t, :],
                                               ALU.mult, ALU.add).then_inc(x2_ready, 1)

            def body(b):
                for s in range(H):
                    scores_there(b, s)
                    if s == 7:
                        statistics_there(b + 2)
                    normalise_probs(*b.head(s - 2))
                    mask_scores(b, s)
                    if s == 7:
                        variance(b + 2)
                    reciprocal_sum(*b.head(s - 1))
                    if s == 0:
                        rope("k", b + 1, 1)
                    if s == 1:
                        padding(b + 1)
                    if s in (2, 4):
                        rope("q", b + 1, s // 2 - 1)
                    if s == 3:
                        build_mask(b + 1)
                    if s in (2, 6):
                        split_out(b + -1, 2 + s // 4)
                    if s in (4, 6):
                        split_transposed("k", b + 1, (s - 4) // 2, kt_hi, kt_lo)
                    if s == 5:
                        statistics(b + 2)
                    if s in (8, 10):
                        split_transposed("q", b + 1, (s - 8) // 2, qt_hi, qt_lo)
                    if s == 9:
                        round_ctx(b + 2)
                    if s in (10, 12):
                        add_residual(b + -1, (s - 10) // 2)
                    if s in (12, 14):
                        split_out(b, (s - 12) // 2)
                    if s in (13, 15):
                        split_transposed("x", b + 2, (s - 13) // 2, xnt_hi, xnt_lo)
                    if s == 14:
                        rope("k", b + 2, 0)

            names = list(weights)
            dve.wait_ge(consts_loaded, 16 * CONSTS)
            for n in range(2):
                split_weight(n, names[n])
            body(Batch(-1, 0))
            for n in range(2, 4):
                split_weight(n, names[n])
            body(Batch(-1, 1))
            each_batch(dve, body)
            body(Batch(B // 2, 0))

        @block.tensor
        def _(pe):
            def passes(out, hi, lo, w, halves):
                steps = [(st, mv, k) for k in range(KT)
                         for st, mv in ((hi, w_hi[w]), (hi, w_lo[w]), (lo, w_hi[w]))]
                n = len(steps)
                at = {"first": range(n // 2), "second": range(n // 2, n), "all": range(n)}[halves]
                for i in at:
                    st, mv, k = steps[i]
                    last = nc.tensor.matmul(out[:, :], st(k), mv[:, k, :], start=(i == 0), stop=(i == n - 1))
                return last

            def project(name, b, t, halves="all"):
                if not b.exists:
                    return
                if halves != "second":
                    if name == "k":
                        pe.wait_ge(weight_split, 1)
                        pe.wait_ge(ctx_split, b.count(1, 1))
                        pe.wait_ge(x2_ready, (b + -3).count(TT, t + 1))
                    elif name == "q":
                        pe.wait_ge(weight_split, 2)
                        pe.wait_ge(split["x"], b.count(2, 2))
                        pe.wait_ge(rope_read["k"], b.count(TT, t + 1))
                    elif name == "v":
                        pe.wait_ge(weight_split, 3)
                        pe.wait_ge(rope_read["q"], b.count(TT, t + 1))
                    else:
                        pe.wait_ge(weight_split, 4)
                        pe.wait_ge(out_split, b.count(KT, KT))
                        if (b + 2).exists:
                            pe.wait_ge(v_copied, (b + 2).count(TT, t + 1))
                        else:
                            pe.wait_ge(x2_ready, (b + -1).count(TT, t + 1))
                src = {"q": (xnt_hi, xnt_lo), "k": (ctx_hi, ctx_lo), "v": (ctx_hi, ctx_lo), "o": (ot_hi, ot_lo)}[name]
                hi, lo = ((lambda k, a=a: a[:, k, t * P:(t + 1) * P]) for a in src)
                last = passes(proj_ps[t], hi, lo, name, halves)
                if halves != "first":
                    last.then_inc(projected[name], 1)
                elif name == "o" and t == TT - 1:
                    last.then_inc(out_half_read, 1)

            def transpose(name, b, u):
                if not b.exists:
                    return
                if name == "x":
                    pe.wait_ge(split["x"] if u else split["q"], b.count(2, u) if u else b.count(2, 0))
                    pe.wait_ge(xn_ready, b.count(TT, TT))
                    src = xn
                else:
                    before = {"k": "x", "q": "k"}[name]
                    pe.wait_ge(split[name] if u else split[before], b.count(2, 1) if u else b.count(2, 2))
                    pe.wait_ge(rope_added[name], b.count(TT, TT))
                    src = roped[name]
                for k in range(2):
                    for t in range(TT):
                        at = (k * TT + t) * P
                        last = nc.tensor.transpose(tr_ps[:, at:at + P], src[:, t, (2 * u + k) * P:(2 * u + k + 1) * P],
                                                   identity[:, :])
                last.then_inc(transposed[name], 1)

            def score(b, h):
                if not b.exists:
                    return
                if h == 0:
                    pe.wait_ge(k_stacked, b.count(16 * STACK_DMAS, 16 * STACK_DMAS))
                if h % (H // 2) == 0:
                    pe.wait_ge(q_stacked[h // (H // 2)], b.count(16 * STACK_DMAS, 16 * STACK_DMAS))
                pe.wait_ge(masked, b.count(H, h - 1))
                bank = score_ps[h % 2]
                nc.tensor.matmul(bank[:, 0:P], q_stack[:, h, 0:P], k_stack[:, b.c, h, 0:P], start=True, stop=True)
                nc.tensor.matmul(bank[:, P:3 * P], q_stack[:, h, P:2 * P], k_stack[:, b.c, h, :],
                                 start=True, stop=True).then_inc(scored, 1)

            def transpose_probs(b, h):
                if not b.exists:
                    return
                pe.wait_ge(probt_copied, b.count(H, h))
                pe.wait_ge(normed, b.count(H, h + 1))
                for k in range(3):
                    last = nc.tensor.transpose(probt_ps[:, k * P:(k + 1) * P], prob[:, h % 4, k * P:(k + 1) * P], identity[:, :])
                last.then_inc(prob_transposed, 1)

            def product(b, h):
                if not b.exists:
                    return
                g, q = divmod(h, HG)
                if q == 0:
                    pe.wait_ge(out_split, b.count(KT, g - 1))
                    pe.wait_ge(v_copied, b.count(TT, TT))
                pe.wait_ge(probt_copied, b.count(H, h + 1))
                bank = out_ps[g % 2]
                rows = slice(q * DH, (q + 1) * DH)
                nc.tensor.matmul(bank[rows, 0:S], v_sb[:, b.c, 0, h * DH:(h + 1) * DH], probt[:, h % 2, 0:S], start=True, stop=False)
                nc.tensor.matmul(bank[rows, P:S], v_sb[:, b.c, 1, h * DH:(h + 1) * DH], probt[:, h % 2, S:3 * P],
                                 start=False, stop=True).then_inc(pv_done, 1)

            def body(b):
                for s in range(H):
                    score(*b.head(s + 1))
                    product(*b.head(s - 5))
                    transpose_probs(*b.head(s - 3))
                    if s in (3, 5):
                        transpose("k", b + 1, (s - 3) // 2)
                    if s in (7, 9):
                        transpose("q", b + 1, (s - 7) // 2)
                    if s in (12, 14):
                        transpose("x", b + 2, (s - 12) // 2)
                    name, row = (("q", b + 1), ("v", b + 1), ("o", b + -1), ("k", b + 2))[s // 4]
                    project(name, row, s % 4 // 2, ("first", "second")[s % 2])

            pe.wait_ge(consts_loaded, 16 * CONSTS)
            for c in range(2):
                body(Batch(-1, c))
            each_batch(pe, body)
            body(Batch(B // 2, 0))


def ffn_phase(nc, x2_dram, g_ffn, w_gate_t, w_up_t, w_down_t, ident, out_dram):
    with ExitStack() as ctx:
        def sb(name, shape, dt=F32):
            return ctx.enter_context(nc.sbuf_tensor(name, shape, dt))

        def pb(name):
            return ctx.enter_context(nc.psum_tensor(name, [P, 512], F32))

        def sem(name):
            return ctx.enter_context(nc.semaphore(name))

        WG, WU, WD = 0, 1, 2
        COLS = KT * HID
        w_hi = sb("ffn_hi", [P, 3, COLS], F32R)
        w_lo = sb("ffn_lo", [P, 3, COLS], F32R)
        CHUNK = 1024
        CHUNKS = 3 * COLS // CHUNK
        x2 = sb("x2", [P, 2, TT, D])
        xn = sb("ffn_xn", [P, TT, D])
        xt_hi = sb("ffn_xt_hi", [P, 2, KT, S], F32R)
        xt_lo = sb("ffn_xt_lo", [P, 2, KT, S], F32R)
        identity = sb("ffn_identity", [P, P])
        gate = sb("ffn_gate", [P, 1])
        stats = sb("ffn_stats", [P, TT, 6])
        moments = sb("ffn_moments", [P, TT, 2])
        var_eps = sb("ffn_var_eps", [P, TT])
        rstd = sb("ffn_rstd", [P, TT])
        minus_half = sb("ffn_minus_half", [P, TT])
        th = sb("th", [P, 2, S])
        silu2 = sb("silu2", [P, 2, S])
        hid = sb("hid", [P, 2, S])
        hid_hi = sb("hid_hi", [P, 3, S], F32R)
        hid_lo = sb("hid_lo", [P, 3, S], F32R)
        lo_squares = sb("lo_squares", [P, CHUNKS])
        lo_total = sb("lo_total", [P, 1])
        ones = sb("ffn_ones", [P, 1])
        lo_any = sb("lo_any", [1, 1], I32)

        down_ps = [pb(f"down_ps{t}") for t in range(TT)]
        gu_ps = [pb(f"gu_ps{n}") for n in range(3)]
        tr_ps = [pb(f"ffn_tr_ps{n}") for n in range(2)]

        consts_loaded = sem("ffn_consts_loaded")
        gate_ready = sem("ffn_gate_ready")
        gate_scaled = sem("ffn_gate_scaled")
        w_loaded = [sem(f"w_loaded{n}") for n in range(2)]
        w_float = sem("w_float")
        w_rounded = sem("w_rounded")
        w_split = sem("w_split")
        w_squared = sem("w_squared")
        lo_summed = sem("lo_summed")
        ones_ready = sem("ffn_ones_ready")
        lo_counted = sem("lo_counted")
        lo_flag = sem("lo_flag")
        half_ready = sem("ffn_half_ready")
        x2_loaded = [sem(f"x2_loaded{p}") for p in range(2)]
        stats_ready = sem("ffn_stats_ready")
        moments_ready = sem("ffn_moments_ready")
        var_ready = sem("ffn_var_ready")
        rstd_ready = sem("ffn_rstd_ready")
        xn_ready = sem("ffn_xn_ready")
        x_transposed = sem("ffn_x_transposed")
        x_rounded = sem("ffn_x_rounded")
        x_split = sem("ffn_x_split")
        gu_done = sem("gu_done")
        tanh_done = sem("tanh_done")
        silu_done = sem("silu_done")
        hid_done = sem("hid_done")
        hid_rounded = sem("hid_rounded")
        hid_split = sem("hid_split")
        down_step = sem("down_step")
        y_ready = sem("y_ready")
        y_stored = sem("y_stored")

        w_stage = [x2[:, n, :, :].rearrange("p t d -> p (t d)") for n in range(2)]
        w_f32 = xn[:, :, :].rearrange("p t d -> p (t d)")

        def chunk_of(tensor, n):
            return tensor[:, :, :].rearrange("p w c -> p (w c)")[:, n * CHUNK:(n + 1) * CHUNK]

        def chunk_source(n):
            w, at = divmod(n * CHUNK, COLS)
            if w < WD:
                src = (w_gate_t, w_up_t)[w].rearrange("p k h -> p (k h)")
            else:
                src = w_down_t.rearrange("p k d -> p (k d)")
            return src[:, at:at + CHUNK]

        block = ctx.enter_context(nc.Block())

        @block.sync
        def _(sp):
            sp.dma_start(identity[:, :], ident).then_inc(consts_loaded, 16)
            sp.dma_start(gate[:, :], g_ffn.to_broadcast([P, 1])).then_inc(consts_loaded, 16)
            for n in range(CHUNKS):
                if n >= 2:
                    sp.wait_ge(w_float, n - 1)
                sp.dma_start(w_stage[n % 2].bitcast(I32), chunk_source(n)).then_inc(w_loaded[n % 2], 16)

            def load(b):
                if b.exists:
                    sp.wait_ge(y_stored, (b + -1).count(16, 0))
                    sp.dma_start(x2[:, b.c, :, :], x2_dram[b.row].rearrange("(t p) d -> p t d", p=P)).then_inc(x2_loaded[b.c], 16)

            def store(b):
                sp.wait_ge(y_ready, b.count(TT, TT))
                sp.dma_start(out_dram[b.row].rearrange("(t p) d -> p t d", p=P), x2[:, b.c, :, :]).then_inc(y_stored, 16)

            sp.wait_ge(w_float, CHUNKS)
            load(Batch(0, 0))
            load(Batch(0, 1))

            def body(b):
                if (b + -1).exists:
                    store(b + -1)
                    load(b + 1)

            each_batch(sp, body)
            store(Batch(B // 2 - 1, 1))
            sp.wait_ge(y_stored, 16 * B)

        @block.gpsimd
        def _(pool):
            nc.gpsimd.memset(minus_half[:, :], -0.5).then_inc(half_ready, 1)
            pool.wait_ge(half_ready, 1)

            def inverse_std(b):
                if b.exists:
                    pool.wait_ge(xn_ready, b.count(TT, 0))
                    pool.wait_ge(var_ready, b.count(1, 1))
                    nc.gpsimd.tensor_tensor(rstd[:, :], var_eps[:, :], minus_half[:, :], ALU.pow).then_inc(rstd_ready, 1)

            inverse_std(Batch(0, 0))
            each_batch(pool, lambda b: inverse_std(b + 1))

        @block.scalar
        def _(act):
            act.wait_ge(consts_loaded, 32)
            nc.scalar.activation(gate[:, :], gate[:, :], ACT.Tanh).then_inc(gate_ready, 1)

            def round_x(b, u):
                if b.exists:
                    act.wait_ge(x_transposed, b.count(2, u + 1))
                    nc.scalar.activation(xt_hi[:, b.c, 2 * u:2 * u + 2, :], tr_ps[u][:, :].rearrange("p (k s) -> p k s", k=2),
                                         ACT.Copy).then_inc(x_rounded, 1)

            def tanh(b, k):
                act.wait_ge(silu_done, b.count(HT, k - 1))
                act.wait_ge(gu_done, b.count(HT, k + 1))
                nc.scalar.activation(th[:, k % 2, :], gu_ps[k % 3][:, 0:S], ACT.Tanh, scale=0.5 * DEQ).then_inc(tanh_done, 1)

            def round_hidden(b, k):
                act.wait_ge(down_step, b.count(HT, k - 2))
                act.wait_ge(hid_done, b.count(HT, k + 1))
                nc.scalar.activation(hid_hi[:, k % 3, :], hid[:, k % 2, :], ACT.Copy).then_inc(hid_rounded, 1)

            for u in range(2):
                round_x(Batch(0, 0), u)

            def body(b):
                for k in range(HT):
                    tanh(b, k)
                    if k:
                        round_hidden(b, k - 1)
                    elif (b + -1).exists:
                        round_hidden(b + -1, HT - 1)
                    if k in (7, 9):
                        round_x(b + 1, (k - 7) // 2)

            each_batch(act, body)
            round_hidden(Batch(B // 2 - 1, 1), HT - 1)

        @block.vector
        def _(dve):
            dve.wait_ge(gate_ready, 1)
            nc.vector.tensor_scalar(gate[:, :], gate[:, :], DEQ, None, ALU.mult).then_inc(gate_scaled, 1)
            nc.vector.memset(ones[:, :], 1.0).then_inc(ones_ready, 1)
            for n in range(CHUNKS):
                dve.wait_ge(w_loaded[n % 2], 16 * (n // 2 + 1))
                if n:
                    dve.wait_ge(w_split, n)
                nc.vector.tensor_copy(w_f32, w_stage[n % 2].bitcast(I32)).then_inc(w_float, 1)
                dve.wait_ge(w_float, n + 1)
                nc.vector.tensor_copy(chunk_of(w_hi, n), w_f32).then_inc(w_rounded, 1)
                dve.wait_ge(w_rounded, n + 1)
                nc.vector.tensor_tensor(chunk_of(w_lo, n), w_f32, chunk_of(w_hi, n).bitcast(F32), ALU.subtract).then_inc(w_split, 1)
                dve.wait_ge(w_split, n + 1)
                nc.vector.tensor_tensor_reduce(out=w_f32, in0=chunk_of(w_lo, n).bitcast(F32), in1=chunk_of(w_lo, n).bitcast(F32),
                                               scale=1.0, scalar=0.0, op0=ALU.mult, op1=ALU.add,
                                               accum_out=lo_squares[:, n:n + 1]).then_inc(w_squared, 1)
                dve.wait_ge(w_squared, n + 1)
            nc.vector.reduce_sum(lo_total[:, :], lo_squares[:, :], axis=AX.X).then_inc(lo_summed, 1)
            dve.wait_ge(lo_counted, 1)
            nc.vector.tensor_scalar(lo_any[:, :], down_ps[0][0:1, 0:1], 0.0, None, ALU.is_gt).then_inc(lo_flag, 1)
            dve.wait_ge(gate_scaled, 1)

            def statistics(b):
                if b.exists:
                    dve.wait_ge(x2_loaded[b.c], b.half_count(16))
                    for t in range(TT):
                        last = nc.vector.bn_stats(stats[:, t, :], x2[:, b.c, t, :])
                    last.then_inc(stats_ready, 1)

            def statistics_there(b):
                if b.exists:
                    dve.wait_ge(stats_ready, b.count(1, 1))

            def aggregate(b):
                if b.exists:
                    for t in range(TT):
                        last = nc.vector.bn_aggr(moments[:, t, :], stats[:, t, :])
                    last.then_inc(moments_ready, 1)

            def variance(b):
                if b.exists:
                    dve.wait_ge(moments_ready, b.count(1, 1))
                    nc.vector.tensor_scalar(var_eps[:, :], moments[:, :, 1], EPS, None, ALU.add).then_inc(var_ready, 1)

            def normalise(b, t):
                if b.exists:
                    dve.wait_ge(x_transposed, b.count(2, 0))
                    dve.wait_ge(rstd_ready, b.count(1, 1))
                    nc.vector.tensor_scalar(xn[:, t, :], x2[:, b.c, t, :], moments[:, t, 0:1], rstd[:, t:t + 1],
                                            ALU.subtract, ALU.mult).then_inc(xn_ready, 1)

            def split_x(b, u):
                if b.exists:
                    dve.wait_ge(x_rounded, b.count(2, u + 1))
                    nc.vector.tensor_tensor(xt_lo[:, b.c, 2 * u:2 * u + 2, :], tr_ps[u][:, :].rearrange("p (k s) -> p k s", k=2),
                                            xt_hi[:, b.c, 2 * u:2 * u + 2, :].bitcast(F32), ALU.subtract).then_inc(x_split, 1)

            def silu(b, k):
                dve.wait_ge(tanh_done, b.count(HT, k + 1))
                nc.vector.scalar_tensor_tensor(silu2[:, k % 2, :], th[:, k % 2, :], 1.0, gu_ps[k % 3][:, 0:S],
                                               ALU.add, ALU.mult).then_inc(silu_done, 1)

            def hidden(b, k):
                dve.wait_ge(hid_rounded, b.count(HT, k - 1))
                dve.wait_ge(silu_done, b.count(HT, k + 1))
                nc.vector.scalar_tensor_tensor(hid[:, k % 2, :], silu2[:, k % 2, :], 0.5 * DEQ * DEQ, gu_ps[k % 3][:, S:2 * S],
                                               ALU.mult, ALU.mult).then_inc(hid_done, 1)

            def split_hidden(b, k):
                dve.wait_ge(down_step, b.count(HT, k - 2))
                dve.wait_ge(hid_rounded, b.count(HT, k + 1))
                nc.vector.tensor_tensor(hid_lo[:, k % 3, :], hid[:, k % 2, :], hid_hi[:, k % 3, :].bitcast(F32),
                                        ALU.subtract).then_inc(hid_split, 1)

            def output(b, t):
                dve.wait_ge(down_step, b.count(HT, HT))
                nc.vector.scalar_tensor_tensor(x2[:, b.c, t, :], down_ps[t][:, :], gate[:, 0:1], x2[:, b.c, t, :],
                                               ALU.mult, ALU.add).then_inc(y_ready, 1)

            first = Batch(0, 0)
            statistics(first)
            statistics_there(first)
            aggregate(first)
            variance(first)
            for t in range(TT):
                normalise(first, t)
            for u in range(2):
                split_x(first, u)

            def body(b):
                for k in range(HT):
                    if k == 4:
                        statistics_there(b + 1)
                    silu(b, k)
                    if k:
                        split_hidden(b, k - 1)
                    elif (b + -1).exists:
                        split_hidden(b + -1, HT - 1)
                    hidden(b, k)
                    if k == 2 and (b + -1).exists:
                        for t in range(TT):
                            output(b + -1, t)
                    if k == 3:
                        statistics(b + 1)
                    if k == 4:
                        aggregate(b + 1)
                        variance(b + 1)
                    if k in (5, 6):
                        normalise(b + 1, k - 5)
                    if k in (7, 9):
                        split_x(b + 1, (k - 7) // 2)

            each_batch(dve, body)
            last = Batch(B // 2 - 1, 1)
            split_hidden(last, HT - 1)
            for t in range(TT):
                output(last, t)

        @block.tensor
        def _(pe):
            pe.wait_ge(ones_ready, 1)
            pe.wait_ge(lo_summed, 1)
            nc.tensor.matmul(down_ps[0][0:1, 0:1], lo_total[:, :], ones[:, :], start=True, stop=True).then_inc(lo_counted, 1)
            pe.wait_ge(lo_flag, 1)
            any_lo = pe.value_load(lo_any[0:1, 0:1], min_val=0, max_val=1)

            def gate_up(b, k):
                pe.wait_ge(hid_done, b.count(HT, k - 2))
                if k == 0:
                    pe.wait_ge(x_split, b.count(2, 2))
                for w in (WG, WU):
                    out = gu_ps[k % 3][:, w * S:(w + 1) * S]

                    def cols(weights, i):
                        return weights[:, w, i * HID + k * P:i * HID + (k + 1) * P]

                    for i in range(KT):
                        nc.tensor.matmul(out, cols(w_hi, i), xt_hi[:, b.c, i, :], start=(i == 0), stop=False)
                    with pe.If(any_lo > 0):
                        for i in range(KT):
                            nc.tensor.matmul(out, cols(w_lo, i), xt_hi[:, b.c, i, :], start=False, stop=False)
                    for i in range(KT):
                        last = nc.tensor.matmul(out, cols(w_hi, i), xt_lo[:, b.c, i, :], start=False, stop=(i == KT - 1))
                last.then_inc(gu_done, 1)

            def down(b, k):
                pe.wait_ge(hid_split, b.count(HT, k + 1))
                if k == 0:
                    pe.wait_ge(y_ready, b.count(TT, 0))
                for t in range(TT):
                    tok = slice(t * P, (t + 1) * P)

                    def cols(weights):
                        return weights[:, WD, k * D:(k + 1) * D]

                    nc.tensor.matmul(down_ps[t][:, :], hid_hi[:, k % 3, tok], cols(w_hi), start=(k == 0), stop=False)
                    with pe.If(any_lo > 0):
                        nc.tensor.matmul(down_ps[t][:, :], hid_hi[:, k % 3, tok], cols(w_lo), start=False, stop=False)
                    last = nc.tensor.matmul(down_ps[t][:, :], hid_lo[:, k % 3, tok], cols(w_hi), start=False, stop=(k == HT - 1))
                last.then_inc(down_step, 1)

            def transpose(b, u):
                if b.exists:
                    pe.wait_ge(xn_ready, b.count(TT, TT))
                    pe.wait_ge(x_split, b.count(2, u - 1))
                    for k in range(2):
                        for t in range(TT):
                            at = (k * TT + t) * P
                            last = nc.tensor.transpose(tr_ps[u][:, at:at + P], xn[:, t, (2 * u + k) * P:(2 * u + k + 1) * P],
                                                       identity[:, :])
                    last.then_inc(x_transposed, 1)

            for u in range(2):
                transpose(Batch(0, 0), u)

            def body(b):
                for k in range(HT):
                    gate_up(b, k)
                    if k >= 2:
                        down(b, k - 2)
                    elif (b + -1).exists:
                        down(b + -1, HT - 2 + k)
                    if k in (7, 9):
                        transpose(b + 1, (k - 7) // 2)

            each_batch(pe, body)
            for k in (HT - 2, HT - 1):
                down(Batch(B // 2 - 1, 1), k)


def tables():
    theta = (1.0 / np.float32(ROPE_BASE) ** (np.arange(0, DH, 2, dtype=np.float32) / np.float32(DH))).astype(np.float32)
    angle = np.arange(S, dtype=np.float32)[:, None] * theta[None, :]
    cos = np.repeat(np.cos(angle), 2, axis=1).astype(np.float32)
    sin = np.stack([-np.sin(angle), np.sin(angle)], axis=2).reshape(S, DH).astype(np.float32)
    by_tile = lambda a: np.ascontiguousarray(a.reshape(TT, P, DH).transpose(1, 0, 2))
    seen = np.tril(np.ones((S, S), bool))
    causal = np.where(np.concatenate([seen[0:P, 0:P], seen[P:S, :]], axis=1), 0.0, -BIG).astype(np.float32)
    return {"cos": by_tile(cos), "sin": by_tile(sin), "causal": causal, "ident": np.eye(P, dtype=np.float32)}


def kernel(x, ctx_1024, mask_BxS2_if1, g_xattn, g_ffn, L0_xattn_Wq, L0_xattn_Wk, L0_xattn_Wv, L0_xattn_Wo, L0_xattn_bo,
           L0_ffn_w_gate, L0_ffn_w_up, L0_ffn_w_down):
    import concourse.bacc as bacc
    from concourse.bass_utils import run_bass_kernel_spmd

    def c(a):
        return np.ascontiguousarray(a)

    def tiled(w_t):
        w_t = np.asarray(w_t)
        return c(w_t.reshape(-1, P, w_t.shape[1]).transpose(1, 0, 2))

    arrays = {
        "x": c(x), "ctx_t": c(np.asarray(ctx_1024).transpose(0, 2, 1)), "mask": c(mask_BxS2_if1),
        "g_xattn": c(np.asarray(g_xattn).reshape(1, 1)), "g_ffn": c(np.asarray(g_ffn).reshape(1, 1)),
        "wq_t": c(np.asarray(L0_xattn_Wq).T), "wk_t": c(np.asarray(L0_xattn_Wk).T),
        "wv_t": c(np.asarray(L0_xattn_Wv).T), "wo_t": c(np.asarray(L0_xattn_Wo).T),
        "bo": c(np.asarray(L0_xattn_bo).reshape(1, D)),
        "w_gate_t": tiled(np.asarray(L0_ffn_w_gate).T), "w_up_t": tiled(np.asarray(L0_ffn_w_up).T),
        "w_down_t": tiled(np.asarray(L0_ffn_w_down).T),
        **tables(),
    }
    nc = bacc.Bacc("TRN2", target_bir_lowering=False, num_devices=1)
    d = {n: nc.dram_tensor(f"in_{n}", a.shape, mybir.dt.from_np(a.dtype), kind="ExternalInput").ap() for n, a in arrays.items()}
    x2_dram = nc.dram_tensor("x2_scratch", (B, S, D), F32, kind="Internal").ap()
    out = nc.dram_tensor("out_y", (B, S, D), F32, kind="ExternalOutput").ap()
    attention_phase(nc, d["x"], d["ctx_t"], d["mask"], d["g_xattn"], d["wq_t"], d["wk_t"], d["wv_t"], d["wo_t"], d["bo"],
                    d["cos"], d["sin"], d["causal"], d["ident"], x2_dram)
    ffn_phase(nc, x2_dram, d["g_ffn"], d["w_gate_t"], d["w_up_t"], d["w_down_t"], d["ident"], out)
    r = run_bass_kernel_spmd(nc, [{f"in_{n}": a for n, a in arrays.items()}], core_ids=[0])
    return r.results[0]["out_y"]
```

```python
import math
from contextlib import ExitStack

import numpy as np

import concourse.bass as bass
from concourse import mybir

F32 = mybir.dt.float32
F32R = mybir.dt.float32r
I32 = mybir.dt.int32
ALU = mybir.AluOpType
ACT = mybir.ActivationFunctionType
AX = mybir.AxisListType

P = 128
B, S, D = 32, 256, 512
H, DH = 16, 32
HID = 1536
TT = S // P
KT = D // P
HG = P // DH
HT = HID // P
EPS = 1e-5
SCALE = 1.0 / math.sqrt(DH)
DEQ = float(np.float32(1.0 / 127.0))
STACK = 3 * DH
STACK_DMAS = 3 * HG
ROPE_BASE = 10000.0
BIG = 1.0e30


class Batch:

    def __init__(self, j, c):
        self.j, self.c = j, c

    def __add__(self, d):
        return Batch(self.j + (self.c + d) // 2 if (self.c + d) // 2 else self.j, (self.c + d) % 2)

    @property
    def row(self):
        return self.j * 2 + self.c

    @property
    def exists(self):
        return not isinstance(self.j, int) or 0 <= self.row < B

    @property
    def is_first(self):
        return isinstance(self.j, int) and self.row == 0

    def head(self, h):
        return self + h // H, h % H

    def count(self, per_row, n):
        value = self.row * per_row + n
        return max(value, 0) if isinstance(value, int) else value

    def half_count(self, n):
        return self.j * n + n


def each_batch(eng, body):
    for c in range(2):
        body(Batch(0, c))
    with eng.Fori(1, B // 2 - 1) as j:
        for c in range(2):
            body(Batch(j, c))
    for c in range(2):
        body(Batch(B // 2 - 1, c))


def attention_phase(nc, x, ctx_t, mask, g_xattn, wq_t, wk_t, wv_t, wo_t, bo, cos, sin, causal, ident, x2_dram):
    with ExitStack() as ctx:
        def sb(name, shape, dt=F32):
            return ctx.enter_context(nc.sbuf_tensor(name, shape, dt))

        def pb(name):
            return ctx.enter_context(nc.psum_tensor(name, [P, 512], F32))

        def sem(name):
            return ctx.enter_context(nc.semaphore(name))

        weights = {"k": wk_t, "q": wq_t, "v": wv_t, "o": wo_t}
        w_hi = {n: sb(f"w{n}_hi", [P, KT, D], F32R) for n in weights}
        w_lo = {n: sb(f"w{n}_lo", [P, KT, D], F32R) for n in weights}
        identity = sb("identity", [P, P])
        cos_sb = sb("cos_sb", [P, TT, DH])
        sin_sb = sb("sin_sb", [P, TT, DH])
        causal_sb = sb("causal_sb", [P, 3 * P])
        gate = sb("gate", [P, 1])
        gate_bo = sb("gate_bo", [P, D])
        x_raw = sb("x_raw", [P, TT, D])
        res_room = sb("res_room", [P, 2, TT, D])
        x_res = res_room[:, 0, :, :]
        xnt_hi = sb("xnt_hi", [P, KT, S], F32R)
        xnt_lo = sb("xnt_lo", [P, KT, S], F32R)
        ctx_raw = sb("ctx_raw", [P, KT, S])
        ctx_hi = sb("ctx_hi", [P, KT, S], F32R)
        ctx_lo = sb("ctx_lo", [P, KT, S], F32R)
        stats = sb("stats", [P, TT, 6])
        moments = sb("moments", [P, TT, 2])
        var_eps = sb("var_eps", [P, TT])
        rstd = sb("rstd", [P, TT])
        neg_mean = sb("neg_mean", [P, TT])
        shift = sb("shift", [P, TT])
        minus_half = sb("minus_half", [P, TT])
        roped = {n: sb(f"{n}_roped", [P, TT, D]) for n in "qk"}
        xn = roped["q"]
        rope_sin = sb("rope_sin", [P, D])
        qt_hi = sb("qt_hi", [P, KT, S], F32R)
        qt_lo = sb("qt_lo", [P, KT, S], F32R)
        kt_hi = sb("kt_hi", [P, KT, S], F32R)
        kt_lo = sb("kt_lo", [P, KT, S], F32R)
        q_stack = sb("q_stack", [STACK, H, S], F32R)
        k_stack = sb("k_stack", [STACK, 2, H, S], F32R)
        v_sb = sb("v_sb", [P, 2, TT, D])
        w_stage = [room[:, :, :, :].rearrange("p a b n -> p (a b) n") for room in (v_sb, res_room)]
        mask_int = sb("mask_int", [P, S], I32)
        pad = sb("pad", [P, S])
        mask_sb = sb("mask_sb", [P, 2, 3 * P])
        prob = sb("prob", [P, 4, 3 * P])
        neg_max = sb("neg_max", [P, 4, TT])
        row_sum = sb("row_sum", [P, 4, TT])
        row_rcp = sb("row_rcp", [P, 4, TT])
        probt = sb("probt", [P, 2, 3 * P])
        ot_hi = sb("ot_hi", [P, KT, S], F32R)
        ot_lo = sb("ot_lo", [P, KT, S], F32R)

        proj_ps = [pb(f"proj_ps{t}") for t in range(TT)]
        tr_ps = pb("tr_ps")
        score_ps = [pb(f"score_ps{n}") for n in range(2)]
        probt_ps = pb("probt_ps")
        out_ps = [pb(f"out_ps{n}") for n in range(2)]

        consts_loaded = sem("consts_loaded")
        weight_loaded = [sem(f"w{n}_loaded") for n in weights]
        weight_rounded = sem("weight_rounded")
        weight_split = sem("weight_split")
        gate_ready = sem("gate_ready")
        gate_bo_ready = sem("gate_bo_ready")
        half_ready = sem("half_ready")
        x_loaded = sem("x_loaded")
        ctx_loaded = sem("ctx_loaded")
        mask_loaded = sem("mask_loaded")
        ctx_rounded = sem("ctx_rounded")
        ctx_split = sem("ctx_split")
        res_loaded = sem("res_loaded")
        res_ready = sem("res_ready")
        stats_ready = sem("stats_ready")
        moments_ready = sem("moments_ready")
        var_ready = sem("var_ready")
        rstd_ready = sem("rstd_ready")
        shift_ready = sem("shift_ready")
        xn_ready = sem("xn_ready")
        pad_ready = sem("pad_ready")
        projected = {n: sem(f"{n}_projected") for n in "qkvo"}
        transposed = {n: sem(f"{n}_transposed") for n in "xqk"}
        rounded = {n: sem(f"{n}_rounded") for n in "xqk"}
        split = {n: sem(f"{n}_split") for n in "xqk"}
        rope_read = {n: sem(f"{n}_rope_read") for n in "qk"}
        rope_added = {n: sem(f"{n}_rope_added") for n in "qk"}
        k_stacked = sem("k_stacked")
        q_stacked = [sem(f"q_stacked{u}") for u in range(2)]
        v_copied = sem("v_copied")
        scored = sem("scored")
        masked = sem("masked")
        exp_done = sem("exp_done")
        rcp_done = sem("rcp_done")
        normed = sem("normed")
        prob_transposed = sem("prob_transposed")
        probt_copied = sem("probt_copied")
        pv_done = sem("pv_done")
        out_rounded = sem("out_rounded")
        out_split = sem("out_split")
        out_half_read = sem("out_half_read")
        x2_ready = sem("x2_ready")
        x2_stored = sem("x2_stored")

        CONSTS = 6
        block = ctx.enter_context(nc.Block())

        @block.sync
        def _(sp):
            for dst, src in ((identity, ident), (cos_sb, cos), (sin_sb, sin), (causal_sb, causal)):
                sp.dma_start(dst[:], src).then_inc(consts_loaded, 16)
            sp.dma_start(gate[:, :], g_xattn.to_broadcast([P, 1])).then_inc(consts_loaded, 16)
            sp.dma_start(gate_bo[:, :], bo.to_broadcast([P, D])).then_inc(consts_loaded, 16)

            def load_weight(n):
                if n >= 2:
                    sp.wait_ge(weight_split, n - 1)
                rows = list(weights.values())[n].rearrange("(k p) n -> p k n", p=P)
                sp.dma_start(w_stage[n % 2], rows).then_inc(weight_loaded[n], 16)

            def load_x(b):
                if b.exists:
                    tokens = x[b.row].rearrange("(t p) d -> p t d", p=P)
                    sp.wait_ge(xn_ready, b.count(TT, 0))
                    sp.dma_start(x_raw[:, :, :], tokens).then_inc(x_loaded, 16)

            def load_residual(b):
                if b.exists:
                    tokens = x[b.row].rearrange("(t p) d -> p t d", p=P)
                    sp.wait_ge(x2_stored, b.count(16, 0))
                    sp.dma_start(x_res[:, :, :], tokens).then_inc(res_loaded, 16)

            def load_ctx(b):
                if b.exists:
                    features = ctx_t[b.row].rearrange("(k p) s -> p k s", p=P)
                    sp.wait_ge(ctx_split, b.count(1, 0))
                    sp.dma_start(ctx_raw[:, :, :], features).then_inc(ctx_loaded, 16)

            def load_mask(b):
                if b.exists:
                    keys = mask[bass.ds(b.row, 1), :].to_broadcast([P, S])
                    sp.wait_ge(pad_ready, b.count(1, 0))
                    sp.dma_start(mask_int[:, :], keys).then_inc(mask_loaded, 16)

            def stack_k(b):
                if b.exists:
                    sp.wait_ge(split["k"], b.count(2, 2))
                    dst = k_stack[:, b.c, :, :].rearrange("r (t q) s -> r t q s", q=HG)
                    for block_no, src in enumerate((kt_hi, kt_lo, kt_hi)):
                        for q in range(HG):
                            sp.dma_start(dst[block_no * DH:(block_no + 1) * DH, :, q, :].bitcast(F32),
                                         src[q * DH:(q + 1) * DH, :, :].bitcast(F32)).then_inc(k_stacked, 16)

            def stack_q(b, u):
                if b.exists:
                    if u == 0:
                        sp.wait_ge(split["q"], b.count(2, 2))
                    else:
                        sp.wait_ge(scored, b.count(H, 0))
                    dst = q_stack[:, :, :].rearrange("r (t q) s -> r t q s", q=HG)
                    for block_no, src in enumerate((qt_hi, qt_hi, qt_lo)):
                        for q in range(HG):
                            sp.dma_start(dst[block_no * DH:(block_no + 1) * DH, 2 * u:2 * u + 2, q, :].bitcast(F32),
                                         src[q * DH:(q + 1) * DH, 2 * u:2 * u + 2, :].bitcast(F32)).then_inc(q_stacked[u], 16)

            def store_x2(b):
                if b.exists:
                    tokens = x2_dram[b.row].rearrange("(t p) d -> p t d", p=P)
                    sp.wait_ge(x2_ready, b.count(TT, TT))
                    sp.dma_start(tokens, x_res[:, :, :]).then_inc(x2_stored, 16)

            def body(b):
                load_x(b + 2)
                load_ctx(b + 2)
                load_residual(b + -1)
                stack_q(b, 1)
                stack_k(b + 1)
                stack_q(b + 1, 0)
                load_mask(b + 2)
                store_x2(b + -1)

            load_weight(0)
            body(Batch(-1, 0))
            for n in range(1, len(weights)):
                load_weight(n)
            body(Batch(-1, 1))
            each_batch(sp, body)
            body(Batch(B // 2, 0))
            sp.wait_ge(x2_stored, 16 * B)

        @block.gpsimd
        def _(pool):
            nc.gpsimd.memset(minus_half[:, :], -0.5).then_inc(half_ready, 1)
            pool.wait_ge(half_ready, 1)

            def split_ctx(b):
                if b.exists:
                    pool.wait_ge(projected["v"], b.count(TT, 0))
                    pool.wait_ge(ctx_rounded, b.count(1, 1))
                    nc.gpsimd.tensor_tensor(ctx_lo[:, :, :], ctx_raw[:, :, :], ctx_hi[:, :, :].bitcast(F32),
                                            ALU.subtract).then_inc(ctx_split, 1)

            def inverse_std(b):
                if b.exists:
                    pool.wait_ge(xn_ready, b.count(TT, 0))
                    pool.wait_ge(var_ready, b.count(1, 1))
                    nc.gpsimd.tensor_tensor(rstd[:, :], var_eps[:, :], minus_half[:, :], ALU.pow).then_inc(rstd_ready, 1)
                    pool.wait_ge(rstd_ready, b.count(1, 1))
                    nc.gpsimd.tensor_tensor(shift[:, :], neg_mean[:, :], rstd[:, :], ALU.mult).then_inc(shift_ready, 1)

            def rope_add(name, b, t):
                if b.exists:
                    pool.wait_ge(rope_read[name], b.count(TT, t + 1))
                    nc.gpsimd.tensor_tensor(roped[name][:, t, :], roped[name][:, t, :], rope_sin[:, :],
                                            ALU.add).then_inc(rope_added[name], 1)

            def residual(b):
                if b.exists:
                    pool.wait_ge(gate_bo_ready, 2)
                    pool.wait_ge(res_loaded, b.count(16, 16))
                    nc.gpsimd.tensor_tensor(x_res[:, :, :], x_res[:, :, :], gate_bo[:, :].unsqueeze(1).to_broadcast([P, TT, D]),
                                            ALU.add).then_inc(res_ready, 1)

            def body(b):
                rope_add("k", b + 1, 1)
                for t in range(TT):
                    rope_add("q", b + 1, t)
                residual(b + -1)
                inverse_std(b + 2)
                split_ctx(b + 2)
                rope_add("k", b + 2, 0)

            for c in range(2):
                body(Batch(-1, c))
            each_batch(pool, body)
            body(Batch(B // 2, 0))

        @block.scalar
        def _(act):
            act.wait_ge(consts_loaded, 16 * CONSTS)
            nc.scalar.activation(gate[:, :], gate[:, :], ACT.Tanh).then_inc(gate_ready, 1)

            def round_weight(n):
                name = list(weights)[n]
                act.wait_ge(weight_loaded[n], 16)
                nc.scalar.activation(w_hi[name][:, :, :], w_stage[n % 2], ACT.Copy).then_inc(weight_rounded, 1)

            def exponentials(b, h):
                if not b.exists:
                    return
                n = h % 4
                act.wait_ge(masked, b.count(H, h + 1))
                for t, (lo, hi) in enumerate(((0, P), (P, 3 * P))):
                    last = nc.scalar.activation(prob[:, n, lo:hi], prob[:, n, lo:hi], ACT.Exp, bias=neg_max[:, n, t:t + 1],
                                                scale=-1.0, accum_out=row_sum[:, n, t:t + 1])
                last.then_inc(exp_done, 1)

            def copy_probt(b, h):
                if not b.exists:
                    return
                act.wait_ge(pv_done, b.count(H, h - 1))
                act.wait_ge(prob_transposed, b.count(H, h + 1))
                nc.scalar.activation(probt[:, h % 2, :], probt_ps[:, 0:3 * P], ACT.Copy).then_inc(probt_copied, 1)

            def round_transposed(name, b, u, dst):
                if b.exists:
                    if name == "x":
                        act.wait_ge(projected["q"], b.count(TT, 0))
                    elif name == "k":
                        act.wait_ge(k_stacked, b.count(16 * STACK_DMAS, 0))
                    else:
                        act.wait_ge(q_stacked[u], b.count(16 * STACK_DMAS, 0))
                    act.wait_ge(transposed[name], b.count(2, u + 1))
                    nc.scalar.activation(dst[:, 2 * u:2 * u + 2, :], tr_ps[:, :].rearrange("p (k s) -> p k s", k=2),
                                         ACT.Copy).then_inc(rounded[name], 1)

            def copy_v(b, t):
                if b.exists:
                    act.wait_ge(pv_done, b.count(H, -H))
                    act.wait_ge(projected["v"], b.count(TT, t + 1))
                    nc.scalar.activation(v_sb[:, b.c, t, :], proj_ps[t][:, :], ACT.Copy).then_inc(v_copied, 1)

            def round_out(b, g):
                if not b.exists:
                    return
                if g < 2:
                    act.wait_ge(out_half_read, b.count(1, 0))
                else:
                    act.wait_ge(projected["o"], b.count(TT, 0))
                act.wait_ge(pv_done, b.count(H, HG * g + HG))
                nc.scalar.activation(ot_hi[:, g, :], out_ps[g % 2][:, 0:S], ACT.Copy).then_inc(out_rounded, 1)

            def normalise(b, t):
                if b.exists:
                    act.wait_ge(transposed["q"], b.count(2, 0))
                    act.wait_ge(shift_ready, b.count(1, 1))
                    nc.scalar.activation(xn[:, t, :], x_raw[:, t, :], ACT.Identity, bias=shift[:, t:t + 1],
                                         scale=rstd[:, t:t + 1]).then_inc(xn_ready, 1)

            weight_at = {(-2, 10): 0, (-2, 13): 1, (-1, 3): 2}

            def body(b):
                for s in range(H):
                    if not b.exists and (b.row, s) in weight_at:
                        round_weight(weight_at[b.row, s])
                    copy_probt(*b.head(s - 3))
                    exponentials(b, s)
                    if s in (3, 5):
                        round_transposed("k", b + 1, (s - 3) // 2, kt_hi)
                    if s in (7, 9):
                        round_transposed("q", b + 1, (s - 7) // 2, qt_hi)
                    if s in (6, 8):
                        copy_v(b + 1, (s - 6) // 2)
                    if s in (12, 14):
                        round_transposed("x", b + 2, (s - 12) // 2, xnt_hi)
                    if s == 10:
                        for t in range(TT):
                            normalise(b + 2, t)
                    if s in (1, 5):
                        round_out(b + -1, 2 + s // 4)
                    if s in (11, 13):
                        round_out(b, (s - 11) // 2)

            body(Batch(-1, 0))
            body(Batch(-1, 1))
            round_weight(3)
            each_batch(act, body)
            body(Batch(B // 2, 0))

        @block.vector
        def _(dve):
            dve.wait_ge(gate_ready, 1)
            nc.vector.tensor_scalar(gate_bo[:, :], gate_bo[:, :], gate[:, 0:1], None, ALU.mult).then_inc(gate_bo_ready, 2)

            def split_weight(n):
                name = list(weights)[n]
                dve.wait_ge(weight_rounded, n + 1)
                nc.vector.tensor_tensor(w_lo[name][:, :, :], w_stage[n % 2],
                                        w_hi[name][:, :, :].bitcast(F32), ALU.subtract).then_inc(weight_split, 1)

            def statistics(b):
                if b.exists:
                    dve.wait_ge(x_loaded, b.count(16, 16))
                    for t in range(TT):
                        last = nc.vector.bn_stats(stats[:, t, :], x_raw[:, t, :])
                    last.then_inc(stats_ready, 1)

            def statistics_there(b):
                if b.exists:
                    dve.wait_ge(stats_ready, b.count(1, 1))

            def variance(b):
                if b.exists:
                    for t in range(TT):
                        last = nc.vector.bn_aggr(moments[:, t, :], stats[:, t, :])
                    last.then_inc(moments_ready, 1)
                    dve.wait_ge(xn_ready, b.count(TT, 0))
                    dve.wait_ge(moments_ready, b.count(1, 1))
                    nc.vector.tensor_scalar(neg_mean[:, :], moments[:, :, 0], -1.0, None, ALU.mult)
                    nc.vector.tensor_scalar(var_eps[:, :], moments[:, :, 1], EPS, None, ALU.add).then_inc(var_ready, 1)

            def split_transposed(name, b, u, hi, lo):
                if b.exists:
                    dve.wait_ge(rounded[name], b.count(2, u + 1))
                    nc.vector.tensor_tensor(lo[:, 2 * u:2 * u + 2, :], tr_ps[:, :].rearrange("p (k s) -> p k s", k=2),
                                            hi[:, 2 * u:2 * u + 2, :].bitcast(F32), ALU.subtract).then_inc(split[name], 1)

            def rope_cos(name, b, t):
                if b.exists:
                    if t:
                        dve.wait_ge(rope_added[name], b.count(TT, t))
                    elif name == "q":
                        dve.wait_ge(rope_added["k"], b.count(TT, TT))
                    else:
                        dve.wait_ge(rope_added["q"], b.count(TT, 0))
                    dve.wait_ge(transposed[name], b.count(2, 0))
                    dve.wait_ge(projected[name], b.count(TT, t + 1))
                    table = cos_sb[:, t, :].unsqueeze(1).to_broadcast([P, H, DH])
                    nc.vector.tensor_tensor(roped[name][:, t, :].rearrange("p (h d) -> p h d", h=H),
                                            proj_ps[t][:, :].rearrange("p (h d) -> p h d", h=H), table, ALU.mult)
                    sine_product(t, 0)

            def rope_sin_odd(name, b, t):
                if b.exists:
                    sine_product(t, 1).then_inc(rope_read[name], 1)

            def sine_product(t, e):
                pairs = proj_ps[t][:, :].rearrange("p (h i e) -> p h i e", h=H, e=2)
                signs = sin_sb[:, t, :].rearrange("p (i e) -> p i e", e=2)[:, :, e].unsqueeze(1).to_broadcast([P, H, DH // 2])
                return nc.vector.tensor_tensor(rope_sin[:, :].rearrange("p (h i e) -> p h i e", h=H, e=2)[:, :, :, e],
                                               pairs[:, :, :, 1 - e], signs, ALU.mult)

            def round_ctx(b):
                if b.exists:
                    dve.wait_ge(projected["v"], b.count(TT, 0))
                    dve.wait_ge(ctx_loaded, b.count(16, 16))
                    nc.vector.tensor_copy(ctx_hi[:, :, :], ctx_raw[:, :, :]).then_inc(ctx_rounded, 1)

            def padding(b):
                if b.exists:
                    dve.wait_ge(mask_loaded, b.count(16, 16))
                    nc.vector.tensor_scalar(pad[:, :], mask_int[:, :], 0.0, -BIG, ALU.is_equal, ALU.mult).then_inc(pad_ready, 1)

            def build_mask(b):
                if b.exists:
                    dve.wait_ge(pad_ready, b.count(1, 1))
                    for lo, hi in ((0, P), (P, 3 * P)):
                        nc.vector.scalar_tensor_tensor(mask_sb[:, b.c, lo:hi], pad[:, 0:hi - lo], 1.0,
                                                       causal_sb[:, lo:hi], ALU.mult, ALU.add)

            def scores_there(b, h):
                if not b.exists:
                    return
                dve.wait_ge(prob_transposed, b.count(H, h - 3))
                dve.wait_ge(scored, b.count(H, h + 1))

            def mask_scores(b, h):
                if not b.exists:
                    return
                n = h % 4
                for t, (lo, hi) in enumerate(((0, P), (P, 3 * P))):
                    last = nc.vector.tensor_tensor_reduce(out=prob[:, n, lo:hi], in0=score_ps[h % 2][:, lo:hi],
                                                          in1=mask_sb[:, b.c, lo:hi], scale=-SCALE, scalar=3.0e38, op0=ALU.add,
                                                          op1=ALU.min, accum_out=neg_max[:, n, t:t + 1])
                last.then_inc(masked, 1)

            def reciprocal_sum(b, h):
                if not b.exists:
                    return
                dve.wait_ge(exp_done, b.count(H, h + 1))
                nc.vector.reciprocal(row_rcp[:, h % 4, :], row_sum[:, h % 4, :]).then_inc(rcp_done, 1)

            def normalise_probs(b, h):
                if not b.exists:
                    return
                n = h % 4
                dve.wait_ge(rcp_done, b.count(H, h + 1))
                for t, (lo, hi) in enumerate(((0, P), (P, 3 * P))):
                    last = nc.vector.tensor_scalar(prob[:, n, lo:hi], prob[:, n, lo:hi], row_rcp[:, n, t:t + 1], None, ALU.mult)
                last.then_inc(normed, 1)

            def split_out(b, g):
                if not b.exists:
                    return
                dve.wait_ge(out_rounded, b.count(KT, g + 1))
                nc.vector.tensor_tensor(ot_lo[:, g, :], out_ps[g % 2][:, 0:S], ot_hi[:, g, :].bitcast(F32),
                                        ALU.subtract).then_inc(out_split, 1)

            def add_residual(b, t):
                if not b.exists:
                    return
                dve.wait_ge(res_ready, b.count(1, 1))
                dve.wait_ge(projected["o"], b.count(TT, t + 1))
                nc.vector.scalar_tensor_tensor(x_res[:, t, :], proj_ps[t][:, :], gate[:, 0:1], x_res[:, t, :],
                                               ALU.mult, ALU.add).then_inc(x2_ready, 1)

            weight_at = {(-2, 11): 0, (-2, 14): 1, (-1, 4): 2}

            def body(b):
                for s in range(H):
                    if not b.exists and (b.row, s) in weight_at:
                        split_weight(weight_at[b.row, s])
                    scores_there(b, s)
                    if s == 8:
                        statistics_there(b + 2)
                    normalise_probs(*b.head(s - 2))
                    mask_scores(b, s)
                    if s == 8:
                        variance(b + 2)
                    reciprocal_sum(*b.head(s - 1))
                    if s == 0:
                        rope_cos("k", b + 1, 1)
                    if s == 1:
                        rope_sin_odd("k", b + 1, 1)
                    if s in (2, 4):
                        rope_cos("q", b + 1, s // 2 - 1)
                    if s in (3, 5):
                        rope_sin_odd("q", b + 1, s // 2 - 1)
                    if s in (2, 6):
                        split_out(b + -1, 2 + s // 4)
                    if s in (4, 6):
                        split_transposed("k", b + 1, (s - 4) // 2, kt_hi, kt_lo)
                    if s == 7:
                        statistics(b + 2)
                    if s in (8, 10):
                        split_transposed("q", b + 1, (s - 8) // 2, qt_hi, qt_lo)
                    if s == 9:
                        round_ctx(b + 2)
                        padding(b + 1)
                    if s in (10, 12):
                        add_residual(b + -1, (s - 10) // 2)
                    if s == 11:
                        build_mask(b + 1)
                    if s in (12, 14):
                        split_out(b, (s - 12) // 2)
                    if s in (13, 15):
                        split_transposed("x", b + 2, (s - 13) // 2, xnt_hi, xnt_lo)
                    if s == 14:
                        rope_cos("k", b + 2, 0)
                    if s == 15:
                        rope_sin_odd("k", b + 2, 0)

            dve.wait_ge(consts_loaded, 16 * CONSTS)
            body(Batch(-1, 0))
            body(Batch(-1, 1))
            split_weight(3)
            each_batch(dve, body)
            body(Batch(B // 2, 0))

        @block.tensor
        def _(pe):
            def passes(out, hi, lo, w, half):
                steps = [(st, mv, k) for k in range(KT)
                         for st, mv in ((hi, w_hi[w]), (hi, w_lo[w]), (lo, w_hi[w]))]
                n = len(steps)
                at = {"first": range(n // 2), "second": range(n // 2, n)}[half]
                for i in at:
                    st, mv, k = steps[i]
                    last = nc.tensor.matmul(out[:, :], st(k), mv[:, k, :], start=(i == 0), stop=(i == n - 1))
                return last

            def project(name, b, t, half):
                if not b.exists:
                    return
                if half == "first":
                    if name == "k":
                        pe.wait_ge(weight_split, 1)
                        pe.wait_ge(ctx_split, b.count(1, 1))
                        pe.wait_ge(x2_ready, (b + -3).count(TT, t + 1))
                    elif name == "q":
                        pe.wait_ge(weight_split, 2)
                        pe.wait_ge(split["x"], b.count(2, 2))
                        pe.wait_ge(rope_read["k"], b.count(TT, t + 1))
                    elif name == "v":
                        pe.wait_ge(weight_split, 3)
                        pe.wait_ge(rope_read["q"], b.count(TT, t + 1))
                    else:
                        pe.wait_ge(weight_split, 4)
                        pe.wait_ge(out_split, b.count(KT, KT))
                        if (b + 2).exists:
                            pe.wait_ge(v_copied, (b + 2).count(TT, t + 1))
                        else:
                            pe.wait_ge(x2_ready, (b + -1).count(TT, t + 1))
                src = {"q": (xnt_hi, xnt_lo), "k": (ctx_hi, ctx_lo), "v": (ctx_hi, ctx_lo), "o": (ot_hi, ot_lo)}[name]
                hi, lo = ((lambda k, a=a: a[:, k, t * P:(t + 1) * P]) for a in src)
                last = passes(proj_ps[t], hi, lo, name, half)
                if half == "second":
                    last.then_inc(projected[name], 1)
                elif name == "o" and t == TT - 1:
                    last.then_inc(out_half_read, 1)

            def transpose(name, b, u):
                if not b.exists:
                    return
                if name == "x":
                    pe.wait_ge(split["x"] if u else split["q"], b.count(2, u) if u else b.count(2, 0))
                    pe.wait_ge(xn_ready, b.count(TT, TT))
                    src = xn
                else:
                    before = {"k": "x", "q": "k"}[name]
                    pe.wait_ge(split[name] if u else split[before], b.count(2, 1) if u else b.count(2, 2))
                    pe.wait_ge(rope_added[name], b.count(TT, TT))
                    src = roped[name]
                for k in range(2):
                    for t in range(TT):
                        at = (k * TT + t) * P
                        last = nc.tensor.transpose(tr_ps[:, at:at + P], src[:, t, (2 * u + k) * P:(2 * u + k + 1) * P],
                                                   identity[:, :])
                last.then_inc(transposed[name], 1)

            def score(b, h):
                if not b.exists:
                    return
                if h == 0:
                    pe.wait_ge(k_stacked, b.count(16 * STACK_DMAS, 16 * STACK_DMAS))
                if h % (H // 2) == 0:
                    pe.wait_ge(q_stacked[h // (H // 2)], b.count(16 * STACK_DMAS, 16 * STACK_DMAS))
                pe.wait_ge(masked, b.count(H, h - 1))
                bank = score_ps[h % 2]
                nc.tensor.matmul(bank[:, P:3 * P], q_stack[:, h, P:2 * P], k_stack[:, b.c, h, :], start=True, stop=True)
                nc.tensor.matmul(bank[:, 0:P], q_stack[:, h, 0:P], k_stack[:, b.c, h, 0:P],
                                 start=True, stop=True).then_inc(scored, 1)

            def transpose_probs(b, h):
                if not b.exists:
                    return
                pe.wait_ge(probt_copied, b.count(H, h))
                pe.wait_ge(normed, b.count(H, h + 1))
                for k in range(3):
                    last = nc.tensor.transpose(probt_ps[:, k * P:(k + 1) * P], prob[:, h % 4, k * P:(k + 1) * P], identity[:, :])
                last.then_inc(prob_transposed, 1)

            def product(b, h):
                if not b.exists:
                    return
                g, q = divmod(h, HG)
                if q == 0:
                    pe.wait_ge(out_split, b.count(KT, g - 1))
                    pe.wait_ge(v_copied, b.count(TT, TT))
                pe.wait_ge(probt_copied, b.count(H, h + 1))
                bank = out_ps[g % 2]
                rows = slice(q * DH, (q + 1) * DH)
                nc.tensor.matmul(bank[rows, 0:S], v_sb[:, b.c, 0, h * DH:(h + 1) * DH], probt[:, h % 2, 0:S], start=True, stop=False)
                nc.tensor.matmul(bank[rows, P:S], v_sb[:, b.c, 1, h * DH:(h + 1) * DH], probt[:, h % 2, S:3 * P],
                                 start=False, stop=True).then_inc(pv_done, 1)

            def body(b):
                for s in range(H):
                    score(*b.head(s + 1))
                    product(*b.head(s - 5))
                    transpose_probs(*b.head(s - 3))
                    if s in (3, 5):
                        transpose("k", b + 1, (s - 3) // 2)
                    if s in (7, 9):
                        transpose("q", b + 1, (s - 7) // 2)
                    if s in (12, 14):
                        transpose("x", b + 2, (s - 12) // 2)
                    name, row = (("q", b + 1), ("v", b + 1), ("o", b + -1), ("k", b + 2))[s // 4]
                    project(name, row, s % 4 // 2, ("first", "second")[s % 2])

            pe.wait_ge(consts_loaded, 16 * CONSTS)
            for c in range(2):
                body(Batch(-1, c))
            each_batch(pe, body)
            body(Batch(B // 2, 0))


def ffn_phase(nc, x2_dram, g_ffn, w_ffn, ident, out_dram):
    with ExitStack() as ctx:
        def sb(name, shape, dt=F32):
            return ctx.enter_context(nc.sbuf_tensor(name, shape, dt))

        def pb(name):
            return ctx.enter_context(nc.psum_tensor(name, [P, 512], F32))

        def sem(name):
            return ctx.enter_context(nc.semaphore(name))

        WG, WU, WD = 0, 1, 2
        w_hi = sb("ffn_hi", [P, HT, 3, D], F32R)
        w_lo = sb("ffn_lo", [P, HT, 3, D], F32R)
        w_stage = sb("w_stage", [P, 3, 3, D])
        x2 = sb("x2", [P, 2, TT, D])
        xn = sb("ffn_xn", [P, TT, D])
        xt_hi = sb("ffn_xt_hi", [P, 2, KT, S], F32R)
        xt_lo = sb("ffn_xt_lo", [P, 2, KT, S], F32R)
        identity = sb("ffn_identity", [P, P])
        gate = sb("ffn_gate", [P, 1])
        stats = sb("ffn_stats", [P, TT, 6])
        moments = sb("ffn_moments", [P, TT, 2])
        var_eps = sb("ffn_var_eps", [P, TT])
        rstd = sb("ffn_rstd", [P, TT])
        minus_half = sb("ffn_minus_half", [P, TT])
        th = sb("th", [P, 2, S])
        silu2 = sb("silu2", [P, 2, S])
        hid = sb("hid", [P, 2, S])
        hid_hi = sb("hid_hi", [P, 3, S], F32R)
        hid_lo = sb("hid_lo", [P, 3, S], F32R)
        lo_squares = sb("lo_squares", [P, HT])
        lo_total = sb("lo_total", [P, 1])
        ones = sb("ffn_ones", [P, 1])
        lo_any = sb("lo_any", [1, 1], I32)

        down_ps = [[pb(f"down_ps{c}{t}") for t in range(TT)] for c in range(2)]
        gu_ps = [pb(f"gu_ps{n}") for n in range(3)]
        tr_ps = pb("ffn_tr_ps")

        consts_loaded = sem("ffn_consts_loaded")
        gate_ready = sem("ffn_gate_ready")
        gate_scaled = sem("ffn_gate_scaled")
        w_loaded = [sem(f"w_loaded{n}") for n in range(3)]
        w_float = sem("w_float")
        w_rounded = sem("w_rounded")
        w_split = sem("w_split")
        w_checked = sem("w_checked")
        lo_summed = sem("lo_summed")
        ones_ready = sem("ffn_ones_ready")
        lo_counted = sem("lo_counted")
        lo_flag = sem("lo_flag")
        half_ready = sem("ffn_half_ready")
        x2_loaded = [sem(f"x2_loaded{p}") for p in range(2)]
        stats_ready = sem("ffn_stats_ready")
        moments_ready = sem("ffn_moments_ready")
        var_ready = sem("ffn_var_ready")
        rstd_ready = sem("ffn_rstd_ready")
        xn_ready = sem("ffn_xn_ready")
        x_transposed = sem("ffn_x_transposed")
        x_rounded = sem("ffn_x_rounded")
        x_split = sem("ffn_x_split")
        gu_done = sem("gu_done")
        tanh_done = sem("tanh_done")
        silu_done = sem("silu_done")
        hid_done = sem("hid_done")
        hid_rounded = sem("hid_rounded")
        hid_split = sem("hid_split")
        down_step = sem("down_step")
        y_ready = sem("y_ready")
        y_stored = sem("y_stored")

        block = ctx.enter_context(nc.Block())

        @block.sync
        def _(sp):
            sp.dma_start(identity[:, :], ident).then_inc(consts_loaded, 16)
            sp.dma_start(gate[:, :], g_ffn.to_broadcast([P, 1])).then_inc(consts_loaded, 16)

            def load_weights(k):
                if k >= 3:
                    sp.wait_ge(w_checked, k - 2)
                sp.dma_start(w_stage[:, k % 3, :, :].bitcast(I32), w_ffn[:, k, :, :]).then_inc(w_loaded[k % 3], 16)

            def load(b):
                if b.exists:
                    sp.wait_ge(y_stored, (b + -1).count(16, 0))
                    sp.dma_start(x2[:, b.c, :, :], x2_dram[b.row].rearrange("(t p) d -> p t d", p=P)).then_inc(x2_loaded[b.c], 16)

            def store(b):
                sp.wait_ge(y_ready, b.count(TT, TT))
                sp.dma_start(out_dram[b.row].rearrange("(t p) d -> p t d", p=P), x2[:, b.c, :, :]).then_inc(y_stored, 16)

            load(Batch(0, 0))
            for k in range(3):
                load_weights(k)
            load(Batch(0, 1))
            for k in range(3, HT):
                load_weights(k)

            def body(b):
                if (b + -1).exists:
                    store(b + -1)
                    load(b + 1)

            each_batch(sp, body)
            store(Batch(B // 2 - 1, 1))
            sp.wait_ge(y_stored, 16 * B)

        @block.gpsimd
        def _(pool):
            nc.gpsimd.memset(minus_half[:, :], -0.5).then_inc(half_ready, 1)
            pool.wait_ge(half_ready, 1)

            def inverse_std(b):
                if b.exists:
                    pool.wait_ge(xn_ready, b.count(TT, 0))
                    pool.wait_ge(var_ready, b.count(1, 1))
                    nc.gpsimd.tensor_tensor(rstd[:, :], var_eps[:, :], minus_half[:, :], ALU.pow).then_inc(rstd_ready, 1)

            inverse_std(Batch(0, 0))
            each_batch(pool, lambda b: inverse_std(b + 1))

        @block.scalar
        def _(act):
            act.wait_ge(consts_loaded, 32)
            nc.scalar.activation(gate[:, :], gate[:, :], ACT.Tanh).then_inc(gate_ready, 1)

            def round_x(b, u):
                if b.exists:
                    act.wait_ge(x_transposed, b.count(2, u + 1))
                    nc.scalar.activation(xt_hi[:, b.c, 2 * u:2 * u + 2, :], tr_ps[:, :].rearrange("p (k s) -> p k s", k=2),
                                         ACT.Copy).then_inc(x_rounded, 1)

            def tanh(b, k):
                act.wait_ge(silu_done, b.count(HT, k - 1))
                act.wait_ge(gu_done, b.count(HT, k + 1))
                nc.scalar.activation(th[:, k % 2, :], gu_ps[k % 3][:, 0:S], ACT.Tanh, scale=0.5 * DEQ).then_inc(tanh_done, 1)

            def round_hidden(b, k):
                act.wait_ge(down_step, b.count(HT, k - 2))
                act.wait_ge(hid_done, b.count(HT, k + 1))
                nc.scalar.activation(hid_hi[:, k % 3, :], hid[:, k % 2, :], ACT.Copy).then_inc(hid_rounded, 1)

            def round_weights(k):
                act.wait_ge(w_float, k + 1)
                nc.scalar.activation(w_hi[:, k, :, :], w_stage[:, k % 3, :, :], ACT.Copy).then_inc(w_rounded, 1)

            def check_weights(k):
                act.wait_ge(w_split, k + 1)
                nc.scalar.activation(w_stage[:, k % 3, :, :], w_lo[:, k, :, :].bitcast(F32), ACT.Square,
                                     accum_out=lo_squares[:, k:k + 1]).then_inc(w_checked, 1)

            for u in range(2):
                round_x(Batch(0, 0), u)
                round_weights(u)
            check_weights(0)

            def body(b):
                for k in range(HT):
                    tanh(b, k)
                    if k:
                        round_hidden(b, k - 1)
                    elif (b + -1).exists:
                        round_hidden(b + -1, HT - 1)
                    if b.is_first and k + 2 < HT:
                        round_weights(k + 2)
                    if b.is_first and k + 1 < HT:
                        check_weights(k + 1)
                    if k in (9, 10):
                        round_x(b + 1, k - 9)

            each_batch(act, body)
            round_hidden(Batch(B // 2 - 1, 1), HT - 1)

        @block.vector
        def _(dve):
            dve.wait_ge(gate_ready, 1)
            nc.vector.tensor_scalar(gate[:, :], gate[:, :], DEQ, None, ALU.mult).then_inc(gate_scaled, 1)
            nc.vector.memset(ones[:, :], 1.0).then_inc(ones_ready, 1)

            def float_weights(k):
                dve.wait_ge(w_loaded[k % 3], 16 * (k // 3 + 1))
                nc.vector.tensor_copy(w_stage[:, k % 3, :, :], w_stage[:, k % 3, :, :].bitcast(I32)).then_inc(w_float, 1)

            def split_weights(k):
                dve.wait_ge(w_rounded, k + 1)
                nc.vector.tensor_tensor(w_lo[:, k, :, :], w_stage[:, k % 3, :, :], w_hi[:, k, :, :].bitcast(F32),
                                        ALU.subtract).then_inc(w_split, 1)

            def statistics(b):
                if b.exists:
                    dve.wait_ge(x2_loaded[b.c], b.half_count(16))
                    for t in range(TT):
                        last = nc.vector.bn_stats(stats[:, t, :], x2[:, b.c, t, :])
                    last.then_inc(stats_ready, 1)

            def statistics_there(b):
                if b.exists:
                    dve.wait_ge(stats_ready, b.count(1, 1))

            def aggregate(b):
                if b.exists:
                    for t in range(TT):
                        last = nc.vector.bn_aggr(moments[:, t, :], stats[:, t, :])
                    last.then_inc(moments_ready, 1)

            def variance(b):
                if b.exists:
                    dve.wait_ge(moments_ready, b.count(1, 1))
                    nc.vector.tensor_scalar(var_eps[:, :], moments[:, :, 1], EPS, None, ALU.add).then_inc(var_ready, 1)

            def normalise(b, t):
                if b.exists:
                    dve.wait_ge(x_transposed, b.count(2, 0))
                    dve.wait_ge(rstd_ready, b.count(1, 1))
                    nc.vector.tensor_scalar(xn[:, t, :], x2[:, b.c, t, :], moments[:, t, 0:1], rstd[:, t:t + 1],
                                            ALU.subtract, ALU.mult).then_inc(xn_ready, 1)

            def split_x(b, u):
                if b.exists:
                    dve.wait_ge(x_rounded, b.count(2, u + 1))
                    nc.vector.tensor_tensor(xt_lo[:, b.c, 2 * u:2 * u + 2, :], tr_ps[:, :].rearrange("p (k s) -> p k s", k=2),
                                            xt_hi[:, b.c, 2 * u:2 * u + 2, :].bitcast(F32), ALU.subtract).then_inc(x_split, 1)

            def silu(b, k):
                dve.wait_ge(tanh_done, b.count(HT, k + 1))
                nc.vector.scalar_tensor_tensor(silu2[:, k % 2, :], th[:, k % 2, :], 1.0, gu_ps[k % 3][:, 0:S],
                                               ALU.add, ALU.mult).then_inc(silu_done, 1)

            def hidden(b, k):
                dve.wait_ge(hid_rounded, b.count(HT, k - 1))
                dve.wait_ge(silu_done, b.count(HT, k + 1))
                nc.vector.scalar_tensor_tensor(hid[:, k % 2, :], silu2[:, k % 2, :], 0.5 * DEQ * DEQ, gu_ps[k % 3][:, S:2 * S],
                                               ALU.mult, ALU.mult).then_inc(hid_done, 1)

            def split_hidden(b, k):
                dve.wait_ge(down_step, b.count(HT, k - 2))
                dve.wait_ge(hid_rounded, b.count(HT, k + 1))
                nc.vector.tensor_tensor(hid_lo[:, k % 3, :], hid[:, k % 2, :], hid_hi[:, k % 3, :].bitcast(F32),
                                        ALU.subtract).then_inc(hid_split, 1)

            def output(b, t):
                dve.wait_ge(down_step, b.count(HT, HT))
                nc.vector.scalar_tensor_tensor(x2[:, b.c, t, :], down_ps[b.c][t][:, :], gate[:, 0:1], x2[:, b.c, t, :],
                                               ALU.mult, ALU.add).then_inc(y_ready, 1)

            first = Batch(0, 0)
            statistics(first)
            statistics_there(first)
            aggregate(first)
            variance(first)
            for t in range(TT):
                normalise(first, t)
            float_weights(0)
            split_x(first, 0)
            split_weights(0)
            split_x(first, 1)
            float_weights(1)
            split_weights(1)
            dve.wait_ge(gate_scaled, 1)

            def body(b):
                for k in range(HT):
                    if k == 7:
                        statistics_there(b + 1)
                    if k == 2 and (b + -1).exists:
                        for t in range(TT):
                            output(b + -1, t)
                    if b.is_first and k + 2 < HT:
                        float_weights(k + 2)
                    silu(b, k)
                    if k:
                        split_hidden(b, k - 1)
                    elif (b + -1).exists:
                        split_hidden(b + -1, HT - 1)
                    hidden(b, k)
                    if b.is_first and k + 2 < HT:
                        split_weights(k + 2)
                    if k == 6:
                        statistics(b + 1)
                    if k == 7:
                        aggregate(b + 1)
                        variance(b + 1)
                    if k == 8:
                        for t in range(TT):
                            normalise(b + 1, t)
                    if k in (9, 10):
                        split_x(b + 1, k - 9)
                if b.is_first:
                    dve.wait_ge(w_checked, HT)
                    nc.vector.reduce_sum(lo_total[:, :], lo_squares[:, :], axis=AX.X).then_inc(lo_summed, 1)
                    dve.wait_ge(lo_counted, 1)
                    nc.vector.tensor_scalar(lo_any[:, :], tr_ps[0:1, 0:1], 0.0, None, ALU.is_gt).then_inc(lo_flag, 1)

            each_batch(dve, body)
            last = Batch(B // 2 - 1, 1)
            split_hidden(last, HT - 1)
            for t in range(TT):
                output(last, t)

        @block.tensor
        def _(pe):
            def gate_up(b, k, with_lo):
                pe.wait_ge(hid_done, b.count(HT, k - 2))
                if k == 0:
                    pe.wait_ge(x_split, b.count(2, 2))
                if b.is_first:
                    pe.wait_ge(w_split, k + 1)
                for w in (WG, WU):
                    steps = [(w_hi, xt_hi, i) for i in range(KT)] + [(w_hi, xt_lo, i) for i in range(KT)]
                    if with_lo:
                        steps += [(w_lo, xt_hi, i) for i in range(KT)]
                    for n, (weights, xt, i) in enumerate(steps):
                        last = nc.tensor.matmul(gu_ps[k % 3][:, w * S:(w + 1) * S], weights[:, k, w, i * P:(i + 1) * P],
                                                xt[:, b.c, i, :], start=(n == 0), stop=(n == len(steps) - 1))
                last.then_inc(gu_done, 1)

            def down(b, k, with_lo):
                pe.wait_ge(hid_split, b.count(HT, k + 1))
                if k == 0:
                    pe.wait_ge(y_ready, b.count(TT, -TT))
                for t in range(TT):
                    steps = [(hid_hi, w_hi), (hid_lo, w_hi)] + ([(hid_hi, w_lo)] if with_lo else [])
                    for n, (hid_part, weights) in enumerate(steps):
                        last = nc.tensor.matmul(down_ps[b.c][t][:, :], hid_part[:, k % 3, t * P:(t + 1) * P], weights[:, k, WD, :],
                                                start=(k == 0 and n == 0), stop=(k == HT - 1 and n == len(steps) - 1))
                last.then_inc(down_step, 1)

            def transpose(b, u):
                if b.exists:
                    pe.wait_ge(xn_ready, b.count(TT, TT))
                    pe.wait_ge(x_split, b.count(2, u))
                    for k in range(2):
                        for t in range(TT):
                            at = (k * TT + t) * P
                            last = nc.tensor.transpose(tr_ps[:, at:at + P], xn[:, t, (2 * u + k) * P:(2 * u + k + 1) * P],
                                                       identity[:, :])
                    last.then_inc(x_transposed, 1)

            def row(b, with_lo):
                for k in range(HT):
                    gate_up(b, k, with_lo)
                    if k >= 2:
                        down(b, k - 2, with_lo)
                    elif (b + -1).exists:
                        down(b + -1, HT - 2 + k, with_lo)
                    if k in (9, 10):
                        transpose(b + 1, k - 9)

            pe.wait_ge(consts_loaded, 32)
            for u in range(2):
                transpose(Batch(0, 0), u)
            first = Batch(0, 0)
            row(first, True)
            pe.wait_ge(ones_ready, 1)
            pe.wait_ge(lo_summed, 1)
            nc.tensor.matmul(tr_ps[0:1, 0:1], lo_total[:, :], ones[:, :], start=True, stop=True).then_inc(lo_counted, 1)
            pe.wait_ge(lo_flag, 1)
            any_lo = pe.value_load(lo_any[0:1, 0:1], min_val=0, max_val=1)

            def body(b):
                if not b.is_first:
                    with pe.If(any_lo > 0):
                        row(b, True)
                    with pe.If(any_lo < 1):
                        row(b, False)

            each_batch(pe, body)
            for k in (HT - 2, HT - 1):
                down(Batch(B // 2 - 1, 1), k, True)


def tables():
    theta = (1.0 / np.float32(ROPE_BASE) ** (np.arange(0, DH, 2, dtype=np.float32) / np.float32(DH))).astype(np.float32)
    angle = np.arange(S, dtype=np.float32)[:, None] * theta[None, :]
    cos = np.repeat(np.cos(angle), 2, axis=1).astype(np.float32)
    sin = np.stack([-np.sin(angle), np.sin(angle)], axis=2).reshape(S, DH).astype(np.float32)
    by_tile = lambda a: np.ascontiguousarray(a.reshape(TT, P, DH).transpose(1, 0, 2))
    seen = np.tril(np.ones((S, S), bool))
    causal = np.where(np.concatenate([seen[0:P, 0:P], seen[P:S, :]], axis=1), 0.0, -BIG).astype(np.float32)
    return {"cos": by_tile(cos), "sin": by_tile(sin), "causal": causal, "ident": np.eye(P, dtype=np.float32)}


def kernel(x, ctx_1024, mask_BxS2_if1, g_xattn, g_ffn, L0_xattn_Wq, L0_xattn_Wk, L0_xattn_Wv, L0_xattn_Wo, L0_xattn_bo,
           L0_ffn_w_gate, L0_ffn_w_up, L0_ffn_w_down):
    import concourse.bacc as bacc
    from concourse.bass_utils import run_bass_kernel_spmd

    def c(a):
        return np.ascontiguousarray(a)

    def by_hidden_tile(w):
        return np.asarray(w).reshape(HT, P, KT, P).transpose(3, 0, 2, 1).reshape(P, HT, 1, D)

    down = np.asarray(L0_ffn_w_down).reshape(D, HT, P).transpose(2, 1, 0).reshape(P, HT, 1, D)

    arrays = {
        "x": c(x), "ctx_t": c(np.asarray(ctx_1024).transpose(0, 2, 1)), "mask": c(mask_BxS2_if1),
        "g_xattn": c(np.asarray(g_xattn).reshape(1, 1)), "g_ffn": c(np.asarray(g_ffn).reshape(1, 1)),
        "wq_t": c(np.asarray(L0_xattn_Wq).T), "wk_t": c(np.asarray(L0_xattn_Wk).T),
        "wv_t": c(np.asarray(L0_xattn_Wv).T), "wo_t": c(np.asarray(L0_xattn_Wo).T),
        "bo": c(np.asarray(L0_xattn_bo).reshape(1, D)),
        "w_ffn": c(np.concatenate([by_hidden_tile(L0_ffn_w_gate), by_hidden_tile(L0_ffn_w_up), down], axis=2)),
        **tables(),
    }
    nc = bacc.Bacc("TRN2", target_bir_lowering=False, num_devices=1)
    d = {n: nc.dram_tensor(f"in_{n}", a.shape, mybir.dt.from_np(a.dtype), kind="ExternalInput").ap() for n, a in arrays.items()}
    x2_dram = nc.dram_tensor("x2_scratch", (B, S, D), F32, kind="Internal").ap()
    out = nc.dram_tensor("out_y", (B, S, D), F32, kind="ExternalOutput").ap()
    attention_phase(nc, d["x"], d["ctx_t"], d["mask"], d["g_xattn"], d["wq_t"], d["wk_t"], d["wv_t"], d["wo_t"], d["bo"],
                    d["cos"], d["sin"], d["causal"], d["ident"], x2_dram)
    ffn_phase(nc, x2_dram, d["g_ffn"], d["w_ffn"], d["ident"], out)
    r = run_bass_kernel_spmd(nc, [{f"in_{n}": a for n, a in arrays.items()}], core_ids=[0])
    return r.results[0]["out_y"]
```
